# Optimizing a Trainium2 kernel written in Bass

```python
import numpy as np
import jax
import jax.numpy as jnp

def _softmax(x, axis=-1):
    return jax.nn.softmax(x, axis=axis)

def _gelu(x):
    return jax.nn.gelu(x, approximate=True)

def _silu(x):
    return jax.nn.silu(x)

def _sigmoid(x):
    return jax.nn.sigmoid(x)

def _layernorm(x, axis=-1, eps=1e-05):
    m = jnp.mean(x, axis=axis, keepdims=True)
    v = jnp.var(x, axis=axis, keepdims=True)
    return (x - m) / jnp.sqrt(v + eps)

def _scatter_add(tgt, idx, src, axis=0):
    return tgt.at[idx].add(src)

def _segment_sum(src, seg, n):
    return jax.ops.segment_sum(src, seg, n)
kernel_name = 'mk_gnn_resnorm_d1_gnn_r32_949785'

def setup_inputs(seed: int=0):
    np.random.seed(seed)
    _w = jnp.asarray

    def _rec_inputs():
        import jax
        import jax.numpy as jnp
        _gk = jax.random.key(seed)
        x = -0.0003713 + 1 * jax.random.normal(jax.random.fold_in(_gk, 1), (50000, 256), jnp.float32)
        src = jax.random.randint(jax.random.fold_in(_gk, 2), (25000,), 0, 50000, jnp.int32)
        dst = jax.random.randint(jax.random.fold_in(_gk, 3), (25000,), 0, 50000, jnp.int32)
        _o = jnp.argsort(dst, stable=True)
        src = src[_o]
        dst = dst[_o]
        edge_attr_128 = -5.16925e-05 + 1.00005 * jax.random.normal(jax.random.fold_in(_gk, 11), (25000, 128), jnp.float32)
        return (x, src, dst, edge_attr_128)
    x, src, dst, edge_attr_128 = _rec_inputs()

    def _L0_gnn_setup():
        import jax, jax.numpy as jnp
        import numpy as np
        N_NODES = 50000
        N_EDGES = 25000
        IN_DIM = 256
        OUT_DIM = 256
        HEADS = 1
        EDGE_DIM = 128
        NEG_SLOPE = 0.01
        key = jax.random.key(seed)
        ks = jax.random.split(key, 8)
        x = jax.random.normal(ks[0], (N_NODES, IN_DIM), dtype=jnp.float32)
        edge_index = jax.random.randint(ks[1], (2, N_EDGES), 0, N_NODES, dtype=jnp.int64)
        edge_attr = jax.random.normal(ks[2], (N_EDGES, EDGE_DIM), dtype=jnp.float32)
        hc = HEADS * OUT_DIM
        Wn = jax.random.normal(ks[3], (hc, IN_DIM), dtype=jnp.float32) / np.sqrt(IN_DIM)
        bn = jnp.zeros((hc,), dtype=jnp.float32)
        We = jax.random.normal(ks[4], (hc, EDGE_DIM), dtype=jnp.float32) / np.sqrt(EDGE_DIM)
        be = jnp.zeros((hc,), dtype=jnp.float32)
        attn = jax.random.normal(ks[5], (1, HEADS, OUT_DIM), dtype=jnp.float32) * np.sqrt(2.0 / (HEADS * OUT_DIM + 1))
        return {'x': x, 'edge_index': edge_index, 'edge_attr': edge_attr, 'Wn': Wn, 'bn': bn, 'We': We, 'be': be, 'attn': attn}
    _L0_gnn_all = _L0_gnn_setup()
    _L0_gnn_in = {k: v for k, v in _L0_gnn_all.items() if k in ('Wn', 'bn', 'We', 'be', 'attn')}
    del _L0_gnn_all
    return {'x': x, 'src': src, 'dst': dst, 'edge_attr_128': edge_attr_128, 'L0_gnn_Wn': _L0_gnn_in['Wn'], 'L0_gnn_bn': _L0_gnn_in['bn'], 'L0_gnn_We': _L0_gnn_in['We'], 'L0_gnn_be': _L0_gnn_in['be'], 'L0_gnn_attn': _L0_gnn_in['attn']}

def reference(x, src, dst, edge_attr_128, L0_gnn_Wn, L0_gnn_bn, L0_gnn_We, L0_gnn_be, L0_gnn_attn):
    import jax
    import jax.numpy as jnp

    def _L0_gnn_ref(x, edge_index, edge_attr, Wn, bn, We, be, attn):
        import jax, jax.numpy as jnp
        import numpy as np
        N_NODES = 50000
        N_EDGES = 25000
        IN_DIM = 256
        OUT_DIM = 256
        HEADS = 1
        EDGE_DIM = 128
        NEG_SLOPE = 0.01
        N = x.shape[0]
        H, C = (attn.shape[1], attn.shape[2])
        src, dst = (edge_index[0], edge_index[1])
        h = x @ Wn.T + bn
        e = edge_attr @ We.T + be
        xj = h[src].reshape(-1, H, C)
        ee = e.reshape(-1, H, C)
        a = jax.nn.leaky_relu(jnp.sum((xj + ee) * attn, axis=-1), NEG_SLOPE)
        m = jax.ops.segment_max(a, dst, num_segments=N)
        a = jnp.exp(a - m[dst])
        denom = jax.ops.segment_sum(a, dst, num_segments=N)
        a = a / (denom[dst] + 1e-16)
        msg = (xj * a[..., None]).reshape(-1, H * C)
        out = jax.ops.segment_sum(msg, dst, num_segments=N)
        return jax.nn.relu(out)
    edge_index = jnp.stack([src, dst])
    x = _layernorm(x + _L0_gnn_ref(x, edge_index, edge_attr_128, L0_gnn_Wn, L0_gnn_bn, L0_gnn_We, L0_gnn_be, L0_gnn_attn), axis=-1)
    return x

_drawn_inputs = setup_inputs


def setup_inputs(seed=0):
    import zlib

    import numpy as np

    out = dict(_drawn_inputs(seed))
    spreads = {'L0_gnn_bn': (0.0, 0.1), 'L0_gnn_be': (0.0, 2.0)}
    factors = {}
    for name, (base, spread) in spreads.items():
        noise = np.random.default_rng([zlib.crc32(name.encode()), seed]).standard_normal(out[name].shape)
        drawn = base * np.exp(spread * noise) if base else spread * noise
        out[name] = jnp.asarray(drawn.astype(out[name].dtype))
    for name, factor in factors.items():
        out[name] = (out[name] * factor).astype(out[name].dtype)
    return out
```

```python
from contextlib import ExitStack

import numpy as np

import concourse.bass as bass
from concourse import mybir
from concourse.alu_op_type import AluOpType as ALU

F32 = mybir.dt.float32
BF16 = mybir.dt.bfloat16
I32 = mybir.dt.int32
ACT = mybir.ActivationFunctionType
AX = mybir.AxisListType

P = 128
N, D = 50000, 256
E, KE = 25000, 128
KC = D // P
SLOPE = 0.01
EPS = 1e-5
BATCH, GROUP = 28, 4
NBATCH = 14
GROUPS = BATCH // GROUP
TILES = BATCH * NBATCH
LAST_TILE = N // P
LAST_ROWS = N - LAST_TILE * P
LAST_USED = LAST_TILE - (NBATCH - 1) * BATCH + 1
FIRST_COLS = 200
FIRST_ROWS = E // FIRST_COLS
TB, TR = 4, 98
STEP = 16
WROWS = (E - P) // STEP + 2
WMAIN = (WROWS - 1) // 16 * 16
LATE = E - P
FAR = 1 << 20
BIG = 3.0e38
EC = E // P
EREST = E - EC * P
ECH = 5
NECH = EC // ECH
ERING = 6
SCORED = [2] * 9 + [1] * 10
SCORES_END = len(SCORED)
LEAD = 2
LAG_VAR, LAG_POW, LAG_OFFSET = 7, 8, 9
LAG_APPLY = 10
PARTS = 3
JUNK = 6

assert TB * TR == TILES and sum(SCORED) == BATCH and NECH * ECH == EC and LATE % 8 == 0


def stages(*parts):
    at, found = 1, {}
    for name, adds in parts:
        found[name] = at
        at += adds
    found["all"] = at - 1
    return found


MAXIMA = stages(("load", 48), ("gather", 0), ("score", 6), ("spread", 1), ("maximum", 10), ("save", 16))
SUMS = stages(("load", 48), ("gather", 0), ("shift", 3), ("spread", 2), ("match", 6), ("sum", 1),
              ("add", 1), ("save", 0))
MAXIMA_GATHERED, MAXIMA_ROWS = 32, 48
SUMS_GATHERED, SUMS_ROWS = 48, 64
NODES = stages(("load", 32), ("divide", 5), ("turn", 1), ("copy", 1), ("project", 1), ("norm", 5),
               ("root", 1), ("apply", 1), ("save", 16))
NROWS = (N + P - 1) // P * P
EDGE_TILES = E // P


def starts(j):
    return sum(SCORED[:j])


def scored(j):
    return range(starts(j), starts(j + 1)) if 0 <= j < len(SCORED) else ()


def gnn_kernel(nc, x, src, dst, edge, Wn, bn, We, be, attn, out):
    with ExitStack() as ctx:
        def sb(name, shape, dt=F32):
            return ctx.enter_context(nc.sbuf_tensor(name, shape, dt))

        def ps(name, shape, dt=F32):
            return ctx.enter_context(nc.psum_tensor(name, shape, dt))

        def sem(name):
            return ctx.enter_context(nc.semaphore(name))

        def dram(name, shape, dt):
            return nc.dram_tensor(name, shape, dt, kind="Internal")

        ds_table = dram("ds_table", [WROWS, 2 * P], I32)
        c_table = dram("c_table", [WROWS, P], F32)
        c_lin = dram("c_lin", [1, E], F32)
        dwin_dram = dram("dwin_dram", [TILES, P], F32)
        cwin_dram = dram("cwin_dram", [TILES, P], F32)

        max_dram = dram("max_dram", [NROWS, 1], F32)
        sum_dram = dram("sum_dram", [NROWS, D + 1], F32)
        a_lin = dram("a_lin", [E, 1], F32)

        ident = sb("ident", [P, P])
        ones_row = sb("ones_row", [1, P])
        ones_col = sb("ones_col", [P, 1])
        ones_bf = sb("ones_bf", [P, P], BF16)
        ones_sq = sb("ones_sq", [P, P])
        iota_i = sb("iota_i", [P, P], I32)
        iota_f = sb("iota_f", [P, P])
        iota_bf = sb("iota_bf", [P, P], BF16)
        node0_i = sb("node0_i", [P, TB], I32)
        node0 = sb("node0", [P, TB])
        power = sb("power", [P, GROUP])
        u_bc = sb("u_bc", [P, D])
        v_bc = sb("v_bc", [P, KE])
        const_c = sb("const_c", [P, 1])
        WT = sb("WT", [P, KC, D])
        bn6 = sb("bn6", [2 * PARTS, D], BF16)
        pick6 = sb("pick6", [P, 2 * PARTS], BF16)

        Wn_sb = sb("Wn_sb", [P, KC, D])
        We_sb = sb("We_sb", [P, KC, KE])
        attn_c = sb("attn_c", [P, KC])
        attn_rep = sb("attn_rep", [P, KC, P])
        bn_c = sb("bn_c", [P, KC])
        be_c = sb("be_c", [P, KC])
        bne = sb("bne", [P, KC])
        bn_row = sb("bn_row", [1, D])
        bn_rest = sb("bn_rest", [1, 2, D])
        bn_part = sb("bn_part", [1, 2 * PARTS, D], BF16)
        firsts_i = sb("firsts_i", [1, FIRST_ROWS], I32)
        firsts = sb("firsts", [1, FIRST_ROWS])
        below = sb("below", [P, TB, FIRST_COLS], BF16)
        nrows = sb("nrows", [P, TB])
        row_f = sb("row_f", [P, TB])
        row_i = sb("row_i", [P, TB], I32)
        rows_i = sb("rows_i", [P, TB, FIRST_COLS], I32)
        rows_f = sb("rows_f", [P, TB, FIRST_COLS])
        nin = sb("nin", [P, TB])
        start_f = sb("start_f", [P, TB])
        start_i = sb("start_i", [P, TB], I32)
        start_s = sb("start_s", [P, TB], I32)
        start_sf = sb("start_sf", [P, TB])
        late = sb("late", [P, TB])
        win_f = sb("win_f", [P, TB])
        win_i = sb("win_i", [P, TB], I32)
        dsw = sb("dsw", [P, TB, 2 * P], I32)
        dr = sb("dr", [P, TB, P])
        away = sb("away", [P, TB, P])
        far = sb("far", [P, TB, P])
        cw = sb("cw", [P, TB, P])
        order_i = sb("order_i", [P, EC + 1], I32)
        order_f = sb("order_f", [P, EC + 1])
        orest_i = sb("orest_i", [1, EREST], I32)
        orest_f = sb("orest_f", [1, EREST])
        viol = sb("viol", [P, EC])
        vrest = sb("vrest", [1, EREST])
        full = sb("full", [P, 2, TB])
        wrong = sb("wrong", [P, 3])
        wrong1 = sb("wrong1", [1, 1])
        flag = sb("flag", [1, 1], I32)
        ea = sb("ea", [P, ERING, ECH, KE])
        ea_rest = sb("ea_rest", [EREST, KE])
        c_main = sb("c_main", [P, EC])
        c_out = sb("c_out", [P, EC])
        c_rest = sb("c_rest", [EREST, 2])

        drel = sb("drel", [P, TILES])
        srcidx = sb("srcidx", [P, TILES + BATCH], I32)
        dwin = sb("dwin", [BATCH, NBATCH, P])
        cwin = sb("cwin", [BATCH, NBATCH, P])
        cont = sb("cont", [BATCH, NBATCH, P + 1])
        neg = sb("neg", [BATCH, NBATCH, P + 1])
        idx_cur = sb("idx_cur", [P, 2, BATCH], I32)
        drel_cur = sb("drel_cur", [P, 2, BATCH])
        alpha_cur = sb("alpha_cur", [P, 2, BATCH])
        cont_cur = sb("cont_cur", [BATCH, P + 1])
        neg_cur = sb("neg_cur", [BATCH, P + 1])
        score = sb("score", [P, BATCH])
        z = sb("z", [BATCH, P])
        a = sb("a", [BATCH, P])
        runmax = sb("runmax", [BATCH, P])
        segmax = sb("segmax", [BATCH, P])
        shifted = sb("shifted", [BATCH, P])
        w = sb("w", [BATCH, P])
        runsum = sb("runsum", [BATCH, P])
        segsum = sb("segsum", [BATCH, P])
        denom = sb("denom", [BATCH, P])
        rdenom = sb("rdenom", [BATCH, P])
        alpha = sb("alpha", [BATCH, P])

        G = sb("G", [P, 2 * BATCH, D])
        M = sb("M", [P, 4, P])
        F = sb("F", [P, 2 * BATCH, P], BF16)
        bias_on = sb("bias_on", [2 * PARTS, 2, GROUP * P], BF16)
        junk = sb("junk", [P, JUNK, D], BF16)
        AT = sb("AT", [P, 2, KC, P])
        X = sb("X", [P, GROUPS, GROUP, D])
        stats = sb("stats", [P, 4, 6])
        mv = sb("mv", [P, BATCH, 2])
        var_e = sb("var_e", [P, BATCH])
        rstd = sb("rstd", [P, BATCH])
        nmr = sb("nmr", [P, BATCH])

        G_flat = G[:, :, :].rearrange("p a d -> p (a d)")

        def part_of_G(at, n):
            return G_flat[:, at * D:at * D + n]

        gx, old, new = part_of_G(0, D + 1), part_of_G(2, D + 1), part_of_G(4, D + 1)
        same, masked, penalty = part_of_G(6, P), part_of_G(7, P), part_of_G(8, P)
        earlier, least, nothing = part_of_G(9, P), part_of_G(10, NROWS // P), part_of_G(12, D + 1)
        diag, bn_bc, bias = part_of_G(14, 2 * P), part_of_G(15, D), part_of_G(16, D)
        y, xrow = part_of_G(17, D), part_of_G(18, D)
        cols = part_of_G(19, 32)
        (dst_f, score_c, term_c, z_c, a_c, max_old, max_loc, max_new, count_c, taken_c, to_c, shift_c,
         w_c, den_c, rden_c, has_c, var_c, rstd_c) = (cols[:, i:i + 1] for i in range(18))
        mv_c, stats_c = cols[:, 20:22], cols[:, 24:30]
        icols = sb("icols", [P, 3], I32)
        src_i, dst_i, to_i = (icols[:, i:i + 1] for i in range(3))

        A = [ps(f"A{i}", [P, 512]) for i in range(2)]
        R = [ps(f"R{i}", [P, 512]) for i in range(4)]
        pS = ps("pS", [P, 512])
        pC = ps("pC", [P, 512])
        scoreT, alphaT, edges6 = pS[0:BATCH, 0:P], pS[:, P:P + BATCH], pC[0:2 * PARTS, :]

        def projected(j):
            return R[j % 4][:, 0:D]

        s_const = sem("s_const")
        s_iota = sem("s_iota")
        s_wload = sem("s_wload")
        s_first = sem("s_first")
        s_order = sem("s_order")
        s_dst_tab = sem("s_dst_tab")
        s_rows = sem("s_rows")
        s_win = sem("s_win")
        s_dwin = sem("s_dwin")
        s_dwin2 = sem("s_dwin2")
        s_ea = [sem(f"s_ea{i}") for i in range(ERING)]
        s_ea_rest = sem("s_ea_rest")
        s_cstore = sem("s_cstore")
        s_ctab = sem("s_ctab")
        s_cw = sem("s_cw")
        s_cwin = sem("s_cwin")
        s_cwin2 = sem("s_cwin2")
        s_bn6 = sem("s_bn6")
        dve_step = sem("dve_step")
        s_pe0 = sem("s_pe0")
        s_attn = sem("s_attn")
        s_rowidx = sem("s_rowidx")
        s_winidx = sem("s_winidx")
        s_dr = sem("s_dr")
        s_srcm = sem("s_srcm")
        s_srcidx = sem("s_srcidx")
        s_bnp = sem("s_bnp")
        s_wrong = sem("s_wrong")
        s_flag = sem("s_flag")
        s_ttr = sem("s_ttr")
        s_cready = sem("s_cready")
        s_gzero = sem("s_gzero")
        s_WT = sem("s_WT")
        s_idx = sem("s_idx")
        s_gather = [[sem(f"s_gather{h}_{g}") for g in range(GROUPS)] for h in range(2)]
        s_drel = sem("s_drel")
        s_F = sem("s_F")
        s_score = sem("s_score")
        s_edges = sem("s_edges")
        s_bias = sem("s_bias")
        s_masks = sem("s_masks")
        s_masked = sem("s_masked")
        s_scoreT = sem("s_scoreT")
        s_soft = sem("s_soft")
        s_shift = sem("s_shift")
        s_exp = sem("s_exp")
        s_alpha = sem("s_alpha")
        s_alphaT = sem("s_alphaT")
        s_ready = sem("s_ready")
        s_M = sem("s_M")
        s_agg = sem("s_agg")
        s_AT = sem("s_AT")
        s_proj = sem("s_proj")
        s_y = sem("s_y")
        s_stats = sem("s_stats")
        s_mv = sem("s_mv")
        s_var = sem("s_var")
        s_rstd = sem("s_rstd")
        s_offset = sem("s_offset")
        s_apply = sem("s_apply")
        s_xin = [sem(f"s_xin{g}") for g in range(GROUPS)]
        s_xout = [sem(f"s_xout{g}") for g in range(GROUPS)]

        s_clear = sem("s_clear")
        s_maxima = sem("s_maxima")
        s_sums = sem("s_sums")
        s_nodes = sem("s_nodes")
        s_max_rows = sem("s_max_rows")
        s_sum_rows = sem("s_sum_rows")
        CLEAR_SETUP = 7
        CLEARED = CLEAR_SETUP + 16 * (NROWS // P + 1)

        def wait(eng, s, batch, per, extra=0):
            if isinstance(batch, int) and batch * per + extra <= 0:
                return
            eng.wait_ge(s, batch * per + extra)

        def wait_apart(eng, s, batch, per, extra=0):
            if isinstance(batch, int):
                wait(eng, s, batch, per, extra)
                return
            value = eng.to_reg(batch * per + extra)
            eng.wait_ge(s_const, 1)
            eng.wait_ge(s, value)

        def tile_stage(eng, s, plan, t, stage, beyond=0):
            wait_apart(eng, s, t, plan["all"], plan[stage] + beyond)

        def tile_steps(eng, s, plan, t, stage):
            n = [0]

            def step(make):
                tile_stage(eng, s, plan, t, stage, n[0])
                n[0] += 1
                make().then_inc(s, 1)
            return step

        def edge_tiles(eng, tile):
            with eng.Fori(0, EDGE_TILES) as t:
                tile(t, P)
            tile(EDGE_TILES, EREST)

        def node_tiles(eng, tile):
            with eng.Fori(0, LAST_TILE) as t:
                tile(t, P)
            tile(LAST_TILE, LAST_ROWS)

        def rows_at(tensor, t, n):
            return tensor[t * P:t * P + n, :] if isinstance(t, int) else tensor[bass.ds(t * P, n), :]

        def windows_fit(eng):
            eng.wait_ge(s_flag, 1)
            return eng.value_load(flag[0:1, 0:1], min_val=0, max_val=1) == 0

        def batches(eng, iteration):
            iteration(0, 0, 0)
            with eng.Fori(0, NBATCH // 2 - 1) as q:
                iteration(q * 2 + 1, 1, q)
                iteration(q * 2 + 2, 0, q + 1)
            iteration(NBATCH - 1, 1, NBATCH // 2 - 1)

        def group_columns(last, g):
            n = LAST_USED % GROUP if last and g == GROUPS - 1 else GROUP
            at = g % GROUPS * GROUP
            return n, slice(at, at + n)

        def windows_of(tensor):
            t, o = tensor.tensor, tensor.offset
            return [
                (slice(0, WMAIN), bass.AP(tensor=t, offset=o, ap=[[STEP, WMAIN], [1, P]])),
                (slice(WMAIN, WROWS - 1),
                 bass.AP(tensor=t, offset=o + STEP * WMAIN, ap=[[STEP, WROWS - 1 - WMAIN], [1, P]])),
                (slice(WROWS - 1, WROWS), bass.AP(tensor=t, offset=o + LATE, ap=[[P, 1], [1, P]])),
            ]

        def group_rows(tensor, b, g):
            row = (b * BATCH + g * GROUP) * P
            if isinstance(row, int):
                part = tensor[row:row + GROUP * P, :]
            else:
                part = tensor[bass.ds(row, GROUP * P), :]
            return part.rearrange("(a p) d -> p a d", p=P)

        block = ctx.enter_context(nc.Block())

        @block.sync
        def _(sp):
            sp.dma_start(firsts_i[:, :], dst.rearrange("(a r c) -> a r c", a=1, c=FIRST_COLS)[:, :, 0],
                         allow_slow_non_contiguous=True).then_inc(s_first, 16)
            sp.dma_start(attn_c[:, :], attn.rearrange("a h (c p) -> p (a h c)", p=P),
                         allow_slow_non_contiguous=True).then_inc(s_wload, 16)
            sp.dma_start(bn_c[:, :], bn.rearrange("(c p) -> p c", p=P),
                         allow_slow_non_contiguous=True).then_inc(s_wload, 16)
            sp.dma_start(be_c[:, :], be.rearrange("(c p) -> p c", p=P),
                         allow_slow_non_contiguous=True).then_inc(s_wload, 16)
            sp.dma_start(bn_row[:, :], bn.rearrange("(a d) -> a d", a=1)).then_inc(s_wload, 16)
            sp.dma_start(Wn_sb[:, :, :], Wn.rearrange("(c p) k -> p c k", p=P)).then_inc(s_wload, 16)
            sp.dma_start(We_sb[:, :, :], We.rearrange("(c p) k -> p c k", p=P)).then_inc(s_wload, 16)
            main = edge[0:EC * P, :].rearrange("(p e) k -> p e k", e=EC)
            for c in range(NECH):
                if c == 1:
                    sp.dma_start(ea_rest[:, :], edge[EC * P:E, :]).then_inc(s_ea_rest, 16)
                    t, o = dst.tensor, dst.offset
                    sp.dma_start(order_i[:, :], bass.AP(tensor=t, offset=o, ap=[[EC, P], [1, EC + 1]]))\
                        .then_inc(s_order, 16)
                    sp.dma_start(orest_i[:, :], dst.rearrange("(a e) -> a e", a=1)[:, EC * P:E])\
                        .then_inc(s_order, 16)
                if c >= ERING:
                    sp.wait_ge(s_ttr, c - ERING + 1)
                sp.dma_start(ea[:, c % ERING, :, :], main[:, c * ECH:(c + 1) * ECH, :])\
                    .then_inc(s_ea[c % ERING], 16)
            sp.wait_ge(s_bnp, 1)
            for i in range(2 * PARTS):
                sp.dma_start(bn6[i:i + 1, :], bn_part[:, i, :]).then_inc(s_bn6, 16)
            for g in range(GROUPS):
                sp.dma_start(X[:, g, :, :], group_rows(x, 0, g)).then_inc(s_xin[g], 16)

            def load(b, g, known_last):
                if known_last and g == GROUPS - 1:
                    full_rows = (LAST_TILE % GROUP) * P
                    row = (LAST_TILE - LAST_TILE % GROUP) * P
                    sp.dma_start(X[:, g, 0:LAST_TILE % GROUP, :],
                                 x[row:row + full_rows, :].rearrange("(a p) d -> p a d", p=P))\
                        .then_inc(s_xin[g], 16)
                    sp.dma_start(X[0:LAST_ROWS, g, LAST_TILE % GROUP, :], x[LAST_TILE * P:N, :])\
                        .then_inc(s_xin[g], 16)
                else:
                    sp.dma_start(X[:, g, :, :], group_rows(x, b, g)).then_inc(s_xin[g], 16)

            def iteration(b, half, use):
                first, last = isinstance(b, int) and b == 0, isinstance(b, int) and b == NBATCH - 1
                for g in range(GROUPS):
                    short = last and g == GROUPS - 1
                    wait(sp, s_apply, b, BATCH, LAST_USED if short else g * GROUP + GROUP)
                    if short:
                        row = (LAST_TILE - LAST_TILE % GROUP) * P
                        sp.dma_start(out[row:LAST_TILE * P, :].rearrange("(a p) d -> p a d", p=P),
                                     X[:, g, 0:LAST_TILE % GROUP, :]).then_inc(s_xout[g], 16)
                        sp.dma_start(out[LAST_TILE * P:N, :], X[0:LAST_ROWS, g, LAST_TILE % GROUP, :])\
                            .then_inc(s_xout[g], 16)
                    else:
                        sp.dma_start(group_rows(out, b, g), X[:, g, :, :]).then_inc(s_xout[g], 16)
                    if g == 0 and not first:
                        wait(sp, s_xout[GROUPS - 1], b, 16)
                        load(b, GROUPS - 1, last)
                    if g >= 1 and not last:
                        wait(sp, s_xout[g - 1], b, 16, 16)
                        load(b + 1, g - 1, False)

            with sp.If(windows_fit(sp)):
                batches(sp, iteration)
                for g in range(GROUPS):
                    sp.wait_ge(s_xout[g], 16 * (NBATCH + (g == GROUPS - 1)))
            with sp.Else():
                sp.wait_ge(s_clear, CLEAR_SETUP)
                with sp.Fori(0, NROWS // P) as t:
                    sp.dma_start(sum_dram[bass.ds(t * P, P), :], nothing).then_inc(s_clear, 16)
                sp.dma_start(max_dram[:, :].rearrange("(p r) a -> p (r a)", p=P), least)\
                    .then_inc(s_clear, 16)
                sp.wait_ge(s_cstore, 32)
                sp.wait_ge(s_bn6, 16 * 2 * PARTS)
                for g in range(GROUPS):
                    sp.wait_ge(s_xin[g], 16)
                src_rows = src.rearrange("(e a) -> e a", a=1)
                dst_rows = dst.rearrange("(e a) -> e a", a=1)
                term_rows = c_lin[:, :].rearrange("a e -> e a")

                def load(s, t, n, third, into):
                    for rows, to in ((src_rows, src_i), (dst_rows, dst_i), (third, into)):
                        sp.dma_start(to[0:n, :], rows_at(rows, t, n), allow_slow_non_contiguous=True)\
                            .then_inc(s, 16)

                def maxima_tile(t, n):
                    tile_stage(sp, s_maxima, MAXIMA, t, "load")
                    load(s_maxima, t, n, term_rows, term_c)
                    tile_stage(sp, s_maxima, MAXIMA, t, "save")
                    sp.dma_start(rows_at(a_lin, t, n), a_c[0:n, :], allow_slow_non_contiguous=True)\
                        .then_inc(s_maxima, 16)

                def sums_tile(t, n):
                    tile_stage(sp, s_sums, SUMS, t, "load")
                    load(s_sums, t, n, a_lin, a_c)

                def nodes_tile(t, n):
                    tile_stage(sp, s_nodes, NODES, t, "load")
                    sp.dma_start(old[0:n, :], rows_at(sum_dram, t, n)).then_inc(s_nodes, 16)
                    sp.dma_start(xrow[0:n, :], rows_at(x, t, n)).then_inc(s_nodes, 16)
                    tile_stage(sp, s_nodes, NODES, t, "save")
                    sp.dma_start(rows_at(out, t, n), y[0:n, :]).then_inc(s_nodes, 16)

                edge_tiles(sp, maxima_tile)
                edge_tiles(sp, sums_tile)
                node_tiles(sp, nodes_tile)
                sp.wait_ge(s_nodes, NODES["all"] * (LAST_TILE + 1) + 1)

        @block.gpsimd
        def _(pool):
            pool.memset(ident[:, :], 0.0).then_inc(s_iota, 1)
            pool.iota(node0_i[:, :], [[TR * P, TB]], base=0, channel_multiplier=P).then_inc(s_const, 1)
            pool.iota(iota_i[:, :], [[1, P]], base=0, channel_multiplier=0).then_inc(s_const, 1)
            pool.memset(ones_row[:, :], 1.0).then_inc(s_const, 1)
            pool.memset(ones_col[:, :], 1.0).then_inc(s_const, 1)
            pool.memset(ones_bf[:, :], 1.0).then_inc(s_const, 1)
            pool.memset(ones_sq[:, :], 1.0).then_inc(s_const, 1)
            pool.memset(power[:, :], -0.5).then_inc(s_const, 1)
            pool.memset(pick6[:, 0:PARTS], 0.0).then_inc(s_const, 1)
            pool.memset(pick6[:, PARTS:2 * PARTS], 1.0).then_inc(s_const, 1)
            pool.memset(srcidx[:, TILES:TILES + BATCH], FAR).then_inc(s_const, 1)
            pool.wait_ge(s_iota, 1)
            pool.affine_select(out=ident[:, :], in_=ident[:, :], compare_op=ALU.not_equal, fill=1.0,
                               base=0, pattern=[[-1, P]], channel_multiplier=1).then_inc(s_const, 1)
            pool.wait_ge(s_rowidx, 1)
            for k in range(TB):
                pool.indirect_dma_start(
                    rows_i[0:TR, k, :], None, dst.rearrange("(r c) -> r c", c=FIRST_COLS),
                    bass.IndirectOffsetOnAxis(ap=row_i[0:TR, k:k + 1], axis=0),
                    bounds_check=FIRST_ROWS - 1, oob_is_err=False).then_inc(s_rows, 16)
            pool.memset(G[:, 0:BATCH, :], 0.0).then_inc(s_gzero, 1)
            pool.wait_ge(s_winidx, 1)
            pool.wait_ge(s_dst_tab, 96)
            for k in range(TB):
                pool.indirect_dma_start(
                    dsw[0:TR, k, :], None, ds_table[:, :],
                    bass.IndirectOffsetOnAxis(ap=win_i[0:TR, k:k + 1], axis=0),
                    bounds_check=WROWS - 1, oob_is_err=False).then_inc(s_win, 16)
            pool.memset(G[:, BATCH:2 * BATCH, :], 0.0).then_inc(s_gzero, 1)
            pool.wait_ge(s_gzero, 2)
            pool.wait_ge(s_srcidx, 1)

            def copy_indices(b, half):
                if isinstance(b, int):
                    cols = srcidx[:, b * BATCH:(b + 1) * BATCH]
                else:
                    cols = srcidx[:, bass.ds(b * BATCH, BATCH)]
                pool.tensor_copy(idx_cur[:, half, :], cols).then_inc(s_idx, 1)

            def gather(half, j):
                pool.indirect_dma_start(
                    G[:, half * BATCH + j, :], None, x,
                    bass.IndirectOffsetOnAxis(ap=idx_cur[:, half, j:j + 1], axis=0),
                    bounds_check=N - 1, oob_is_err=False).then_inc(s_gather[half][j // GROUP], 16)

            for b in range(2):
                copy_indices(b, b)
                pool.wait_ge(s_idx, b + 1)
                for j in range(BATCH):
                    gather(b, j)
                if b == 0:
                    pool.wait_ge(s_ctab, 48)
                    for k in range(TB):
                        pool.indirect_dma_start(
                            cw[0:TR, k, :], None, c_table[:, :],
                            bass.IndirectOffsetOnAxis(ap=win_i[0:TR, k:k + 1], axis=0),
                            bounds_check=WROWS - 1, oob_is_err=False).then_inc(s_cw, 16)

            def iteration(b, half, use):
                first, last = isinstance(b, int) and b == 0, isinstance(b, int) and b == NBATCH - 1
                for j in range(BATCH + LAG_POW if last else BATCH):
                    if not last:
                        wait_apart(pool, s_agg, b, BATCH, j + 1)
                        if j == 0:
                            copy_indices(b + 2, half)
                            wait_apart(pool, s_idx, b, 1, 3)
                        gather(half, j)
                    g = (j - LAG_POW) // GROUP
                    n, cols = group_columns(last, g)
                    if (j - LAG_POW) % GROUP == 0 and (g >= 0 or not first) and g < GROUPS:
                        wait(pool, s_var, b, GROUPS, g + 1)
                        pool.tensor_tensor(rstd[:, cols], var_e[:, cols], power[:, 0:n], ALU.pow)\
                            .then_inc(s_rstd, 1)

            with pool.If(windows_fit(pool)):
                batches(pool, iteration)
                for g in range(GROUPS):
                    pool.wait_ge(s_gather[0][g], 16 * GROUP * (NBATCH // 2 + 1))
                    pool.wait_ge(s_gather[1][g], 16 * GROUP * (NBATCH // 2))
            with pool.Else():
                for g in range(GROUPS):
                    pool.wait_ge(s_gather[0][g], 16 * GROUP)
                    pool.wait_ge(s_gather[1][g], 16 * GROUP)
                pool.memset(nothing, 0.0).then_inc(s_clear, 1)
                pool.memset(least, -BIG).then_inc(s_clear, 1)
                pool.memset(cols, 0.0).then_inc(s_clear, 1)
                pool.memset(gx[:, D:D + 1], 1.0).then_inc(s_clear, 1)

                def rows_of(s, to, table, index, n):
                    pool.indirect_dma_start(
                        to[0:n, :], None, table, bass.IndirectOffsetOnAxis(ap=index[0:n, :], axis=0),
                        bounds_check=N - 1, oob_is_err=False).then_inc(s, 16)

                def rows_to(s, table, index, of, n):
                    pool.indirect_dma_start(
                        table, bass.IndirectOffsetOnAxis(ap=index[0:n, :], axis=0), of[0:n, :], None,
                        bounds_check=N - 1, oob_is_err=False).then_inc(s, 16)

                def maxima_tile(t, n):
                    tile_stage(pool, s_maxima, MAXIMA, t, "gather")
                    rows_of(s_max_rows, gx[:, 0:D], x, src_i, n)
                    rows_of(s_max_rows, max_old, max_dram[:, :], dst_i, n)
                    tile_stage(pool, s_maxima, MAXIMA, t, "save")
                    rows_to(s_max_rows, max_dram[:, :], to_i, max_new, n)
                    wait_apart(pool, s_max_rows, t, MAXIMA_ROWS, MAXIMA_ROWS)

                def sums_tile(t, n):
                    tile_stage(pool, s_sums, SUMS, t, "gather")
                    rows_of(s_sum_rows, gx[:, 0:D], x, src_i, n)
                    rows_of(s_sum_rows, max_old, max_dram[:, :], dst_i, n)
                    rows_of(s_sum_rows, old, sum_dram[:, :], dst_i, n)
                    tile_stage(pool, s_sums, SUMS, t, "save")
                    rows_to(s_sum_rows, sum_dram[:, :], to_i, new, n)
                    wait_apart(pool, s_sum_rows, t, SUMS_ROWS, SUMS_ROWS)

                def nodes_tile(t, n):
                    tile_stage(pool, s_nodes, NODES, t, "root")
                    pool.tensor_tensor(rstd_c[0:n, :], var_c[0:n, :], power[0:n, 0:1], ALU.pow)\
                        .then_inc(s_nodes, 1)

                pool.wait_ge(s_clear, CLEARED)
                pool.memset(mv_c, 0.0).then_inc(s_maxima, 1)
                edge_tiles(pool, maxima_tile)
                pool.wait_ge(s_maxima, MAXIMA["all"] * (EDGE_TILES + 1) + 1)
                pool.memset(mv_c, 0.0).then_inc(s_sums, 1)
                edge_tiles(pool, sums_tile)
                pool.wait_ge(s_sums, SUMS["all"] * (EDGE_TILES + 1) + 1)
                pool.memset(mv_c, 0.0).then_inc(s_nodes, 1)
                node_tiles(pool, nodes_tile)

        @block.scalar
        def _(act):
            for i, values in enumerate((dst, src)):
                for rows, part in windows_of(values):
                    act.dma_start(ds_table[rows, i * P:(i + 1) * P], part).then_inc(s_dst_tab, 16)
            act.wait_ge(s_pe0, 5)
            act.copy(WT[:, :, :], R[0][:, :].rearrange("p (c d) -> p c d", c=KC)).then_inc(s_WT, 1)
            act.wait_ge(s_dr, 1)
            act.dma_start(dwin_dram[:, :].rearrange("(k p) e -> p k e", p=TR), dr[0:TR, :, :])\
                .then_inc(s_dwin, 16)
            act.wait_ge(s_dwin, 16)
            act.dma_start(dwin[:, :, :], dwin_dram[:, :].rearrange("(b p) e -> p b e", p=BATCH))\
                .then_inc(s_dwin2, 16)
            act.wait_ge(s_cready, 2)
            act.dma_start(c_lin[:, 0:EC * P].rearrange("a (p e) -> p (a e)", e=EC), c_out[:, :])\
                .then_inc(s_cstore, 16)
            act.dma_start(c_lin[:, EC * P:E].rearrange("a (p e) -> p (a e)", e=1), c_rest[:, 1:2],
                          allow_slow_non_contiguous=True).then_inc(s_cstore, 16)
            act.wait_ge(s_cstore, 32)
            for rows, part in windows_of(c_lin[:, :]):
                act.dma_start(c_table[rows, :], part).then_inc(s_ctab, 16)
            act.wait_ge(s_cw, 16 * TB)
            act.dma_start(cwin_dram[:, :].rearrange("(k p) e -> p k e", p=TR), cw[0:TR, :, :])\
                .then_inc(s_cwin, 16)
            act.wait_ge(s_cwin, 16)
            act.dma_start(cwin[:, :, :], cwin_dram[:, :].rearrange("(b p) e -> p b e", p=BATCH))\
                .then_inc(s_cwin2, 16)

            def masks(b):
                wait(act, s_alpha, b, 1)
                for t, cur in ((neg, neg_cur), (cont, cont_cur)):
                    if isinstance(b, int):
                        part = t[:, b, :]
                    else:
                        part = t[:, bass.ds(b, 1), :].rearrange("p a e -> p (a e)")
                    act.copy(cur[:, :], part).then_inc(s_masked, 1)

            def exponentials(b):
                wait(act, s_shift, b, 1, 1)
                act.activation(w[:, :], shifted[:, :], ACT.Exp).then_inc(s_exp, 1)

            def evacuate(b, j):
                wait(act, s_agg, b, BATCH, j + 1)
                wait(act, s_proj, b, BATCH, j - 1)
                act.copy(AT[:, j % 2, :, :], A[j % 2][:, 0:D].rearrange("p (c n) -> p c n", c=KC))\
                    .then_inc(s_AT, 1)

            def weights(b, half, j):
                if j == 0 or j == BATCH:
                    wait(act, s_ready, b, 1, 1 + j // BATCH)
                wait(act, s_agg, b, BATCH, j - 3)
                k = j % BATCH
                act.activation(M[:, j % 4, :], F[:, half * BATCH + k, :], ACT.Copy,
                               scale=alpha_cur[:, half, k:k + 1]).then_inc(s_M, 1)

            def bias_rows(b, half, g):
                wait(act, s_edges, b, GROUPS, g + 1)
                wait(act, s_proj, b, BATCH, (g - 1) * GROUP)
                act.activation(bias_on[:, (half + g) % 2, :], edges6, ACT.Relu, bias=1.0, scale=-1.0)\
                    .then_inc(s_bias, 1)

            def iteration(b, half, use):
                first, last = isinstance(b, int) and b == 0, isinstance(b, int) and b == NBATCH - 1
                tiles = LAST_USED if last else BATCH
                for j in range(LAST_USED + LAG_APPLY if last else BATCH):
                    if j == SCORES_END - 2 and not last:
                        masks(b + 1)
                    if j == SCORES_END + 3 and not last:
                        exponentials(b + 1)
                    if j + LEAD < tiles or not last:
                        weights(b, half if j + LEAD < BATCH else 1 - half, j + LEAD)
                    if j + 1 < tiles or not last:
                        evacuate(b, j + 1)
                    if j - LAG_APPLY >= 0 or not first:
                        t = (j - LAG_APPLY) % BATCH
                        if t % GROUP == 0:
                            wait(act, s_offset, b, GROUPS, (j - LAG_APPLY) // GROUP + 1)
                        tile = X[:, t // GROUP, t % GROUP, :]
                        act.activation(tile, tile, ACT.Identity, bias=nmr[:, t:t + 1],
                                       scale=rstd[:, t:t + 1]).then_inc(s_apply, 1)
                    if j % GROUP == 1 and (j < 24 or not last):
                        bias_rows(b, half, j // GROUP + 1)

            with act.If(windows_fit(act)):
                act.wait_ge(s_masks, 1)
                masks(0)
                exponentials(0)
                weights(0, 0, 0)
                weights(0, 0, 1)
                bias_rows(0, 0, 0)
                evacuate(0, 0)
                batches(act, iteration)
            with act.Else():
                def sums_tile(t, n):
                    tile_stage(act, s_sums, SUMS, t, "spread")
                    act.activation(w_c[0:n, :], shift_c[0:n, :], ACT.Exp).then_inc(s_sums, 1)

                edge_tiles(act, sums_tile)

        @block.tensor
        def _(pe):
            def dot(o, lhs, rhs, done=None):
                for c in range(KC):
                    mm = pe.matmul(o, lhs[:, c, :], rhs[:, c, :], start=(c == 0), stop=(c == KC - 1))
                mm.then_inc(s_pe0, 1)

            pe.wait_ge(s_const, 11)
            pe.wait_ge(s_attn, 1)
            pe.matmul(R[1][:, 0:FIRST_ROWS], ones_row[:, :], firsts[:, :], start=True, stop=True)\
                .then_inc(s_pe0, 1)
            pe.wait_ge(s_attn, 4)
            dot(A[0][:, 0:KE], attn_rep, We_sb)
            dot(A[1][:, 0:D], attn_rep, Wn_sb)
            for c in range(KC):
                mm = pe.matmul(R[3][:, 0:1], attn_rep[:, c, :], bne[:, c:c + 1], start=(c == 0),
                               stop=(c == KC - 1))
            mm.then_inc(s_pe0, 1)
            for k in range(KC):
                for c in range(KC):
                    mm = pe.transpose(R[0][:, k * D + c * P:k * D + (c + 1) * P],
                                      Wn_sb[:, c, k * P:(k + 1) * P], ident[:, :])
            mm.then_inc(s_pe0, 1)
            pe.wait_ge(s_dr, 1)
            for k in range(TB):
                mm = pe.transpose(pS[:, k * TR:(k + 1) * TR], dr[0:TR, k, :], ident[0:TR, 0:TR])
            mm.then_inc(s_pe0, 1)
            pe.wait_ge(s_srcm, 1)
            for k in range(TB):
                mm = pe.transpose(R[2][:, k * TR:(k + 1) * TR], far[0:TR, k, :], ident[0:TR, 0:TR])
            mm.then_inc(s_pe0, 1)
            pe.wait_ge(s_wrong, 1)
            pe.matmul(R[3][0:1, 4:7], ones_col[:, :], wrong[:, :], start=True, stop=True).then_inc(s_pe0, 1)

            def count_edges(b, half, g):
                wait(pe, s_F, b, BATCH, (g + 1) * GROUP)
                wait(pe, s_bias, b, GROUPS, g)
                first_tile = half * BATCH + g % GROUPS * GROUP
                pe.matmul(edges6, pick6[:, :], F[:, first_tile:first_tile + GROUP, :],
                          start=True, stop=True).then_inc(s_edges, 1)

            def turn_scores(b):
                pe.transpose(scoreT, score[:, :], ident[:, :]).then_inc(s_scoreT, 1)

            def turn_alphas(b):
                pe.transpose(alphaT, alpha[:, :], ident[0:BATCH, 0:BATCH]).then_inc(s_alphaT, 1)

            def aggregate(b, half, j):
                wait(pe, s_M, b, BATCH, j + 1)
                wait(pe, s_AT, b, BATCH, j - 1)
                for c in range(KC):
                    mm = pe.matmul(A[j % 2][:, c * P:(c + 1) * P],
                                   G[:, half * BATCH + j % BATCH, c * P:(c + 1) * P], M[:, j % 4, :],
                                   start=True, stop=True)
                mm.then_inc(s_agg, 1)

            def project(b, half, j):
                wait(pe, s_AT, b, BATCH, j + 1)
                wait(pe, s_y, b, BATCH, j - 3)
                if j % GROUP == 0:
                    wait(pe, s_bias, b, GROUPS, j // GROUP + 1)
                o, at = projected(j), j % GROUP * P
                pe.matmul(o, bias_on[:, (half + j // GROUP) % 2, at:at + P], bn6[:, :],
                          start=True, stop=False)
                for c in range(KC):
                    mm = pe.matmul(o, AT[:, j % 2, c, :], WT[:, c, :], start=False, stop=(c == KC - 1))
                mm.then_inc(s_proj, 1)

            def iteration(b, half, use):
                last = isinstance(b, int) and b == NBATCH - 1
                for j in range(LAST_USED if last else BATCH):
                    if j == SCORES_END and not last:
                        wait(pe, s_score, b, BATCH, 2 * BATCH)
                    if j == SCORES_END + 5 and not last:
                        wait(pe, s_alpha, b, 1, 2)
                    if j % GROUP == 0 and (j < 24 or not last):
                        g = j // GROUP + 1
                        count_edges(b, half if g < GROUPS else 1 - half, g)
                    if j + 1 < LAST_USED or not last:
                        aggregate(b, half if j + 1 < BATCH else 1 - half, j + 1)
                    if j == SCORES_END and not last:
                        turn_scores(b + 1)
                    if j == SCORES_END + 5 and not last:
                        turn_alphas(b + 1)
                    project(b, half, j)

            with pe.If(windows_fit(pe)):
                count_edges(0, 0, 0)
                pe.wait_ge(s_score, BATCH)
                turn_scores(0)
                pe.wait_ge(s_alpha, 1)
                turn_alphas(0)
                pe.wait_ge(s_bn6, 16 * 2 * PARTS)
                pe.wait_ge(s_WT, 1)
                aggregate(0, 0, 0)
                batches(pe, iteration)
            with pe.Else():
                spread, total, turned, projection = A[0], A[1], R[0], R[1]
                pe.wait_ge(s_clear, 4)
                pe.matmul(spread[:, 0:D], ones_row[:, :], bn_row[:, :], start=True, stop=True)\
                    .then_inc(s_clear, 1)

                def maxima_tile(t, n):
                    tile_stage(pe, s_maxima, MAXIMA, t, "spread")
                    pe.matmul(spread[0:n, 0:2 * n], ones_sq[0:n, 0:n], diag[0:n, 0:2 * n], start=True,
                              stop=True).then_inc(s_maxima, 1)

                def sums_tile(t, n):
                    tile_stage(pe, s_sums, SUMS, t, "spread")
                    pe.matmul(spread[0:n, 0:n], ones_sq[0:n, 0:n], diag[0:n, 0:n], start=True,
                              stop=True).then_inc(s_sums, 1)
                    tile_stage(pe, s_sums, SUMS, t, "sum")
                    pe.matmul(total[0:n, 0:D + 1], masked[0:n, 0:n], gx[0:n, :], start=True, stop=True)\
                        .then_inc(s_sums, 1)

                def nodes_tile(t, n):
                    tile_stage(pe, s_nodes, NODES, t, "turn")
                    for c in range(KC):
                        mm = pe.transpose(turned[:, c * P:c * P + n], new[0:n, c * P:(c + 1) * P],
                                          ident[0:n, 0:n])
                    mm.then_inc(s_nodes, 1)
                    tile_stage(pe, s_nodes, NODES, t, "project")
                    for c in range(KC):
                        mm = pe.matmul(projection[0:n, 0:D], AT[:, 0, c, 0:n], WT[:, c, :],
                                       start=(c == 0), stop=(c == KC - 1))
                    mm.then_inc(s_nodes, 1)

                edge_tiles(pe, maxima_tile)
                edge_tiles(pe, sums_tile)
                node_tiles(pe, nodes_tile)

        @block.vector
        def _(dve):
            steps = [0]

            def link(instruction):
                steps[0] += 1
                instruction.then_inc(dve_step, 1)
                dve.wait_ge(dve_step, steps[0])

            dve.wait_ge(s_const, 11)
            dve.tensor_copy(iota_f[:, :], iota_i[:, :]).then_inc(dve_step, 1)
            dve.tensor_copy(iota_bf[:, :], iota_i[:, :]).then_inc(dve_step, 1)
            dve.memset(wrong[:, :], 0.0).then_inc(dve_step, 1)
            dve.memset(cont[:, :, 0:1], 0.0).then_inc(dve_step, 1)
            dve.memset(cont[:, :, P:P + 1], 0.0).then_inc(dve_step, 1)
            steps[0] += 5
            link(dve.tensor_copy(node0[:, :], node0_i[:, :]))
            dve.wait_ge(s_first, 16)
            dve.tensor_copy(firsts[:, :], firsts_i[:, :]).then_inc(s_attn, 1)
            dve.wait_ge(s_wload, 96)
            for c in range(KC):
                dve.tensor_scalar(attn_rep[:, c, :], ones_bf[:, :], attn_c[:, c:c + 1], None, ALU.mult)\
                    .then_inc(s_attn, 1)
            dve.tensor_tensor(bne[:, :], bn_c[:, :], be_c[:, :], ALU.add).then_inc(s_attn, 1)

            def edge_terms(loads):
                for c in loads:
                    dve.wait_ge(s_ea[c % ERING], 16 * (c // ERING + 1))
                    for e in range(ECH):
                        part = ea[:, c % ERING, e, :]
                        ins = dve.tensor_tensor_reduce(
                            out=part, in0=part, in1=v_bc[:, :], scale=1.0, scalar=0.0, op0=ALU.mult,
                            op1=ALU.add, accum_out=c_main[:, c * ECH + e:c * ECH + e + 1])
                    ins.then_inc(s_ttr, 1)

            dve.wait_ge(s_pe0, 1)
            for k in range(TB):
                ins = dve.tensor_scalar(below[0:TR, k, 0:FIRST_ROWS], R[1][0:TR, 0:FIRST_ROWS],
                                        node0[0:TR, k:k + 1], None, ALU.is_lt, ALU.add,
                                        accum_out=nrows[0:TR, k:k + 1])
            link(ins)
            link(dve.tensor_scalar(row_f[0:TR, :], nrows[0:TR, :], -1.0, 0.0, ALU.add, ALU.max))
            dve.tensor_copy(row_i[0:TR, :], row_f[0:TR, :]).then_inc(s_rowidx, 1)
            dve.wait_ge(s_pe0, 4)
            dve.tensor_copy(v_bc[:, :], A[0][:, 0:KE]).then_inc(dve_step, 1)
            dve.tensor_copy(u_bc[:, :], A[1][:, 0:D]).then_inc(dve_step, 1)
            steps[0] += 2
            link(dve.tensor_copy(const_c[:, :], R[3][:, 0:1]))
            link(dve.tensor_copy(bn_part[:, 0, :], bn_row[:, :]))
            link(dve.tensor_tensor(bn_rest[:, 0, :], bn_row[:, :], bn_part[:, 0, :], ALU.subtract))
            link(dve.tensor_copy(bn_part[:, 1, :], bn_rest[:, 0, :]))
            link(dve.tensor_tensor(bn_rest[:, 1, :], bn_rest[:, 0, :], bn_part[:, 1, :], ALU.subtract))
            link(dve.tensor_copy(bn_part[:, 2, :], bn_rest[:, 1, :]))
            dve.tensor_scalar(bn_part[:, PARTS:2 * PARTS, :], bn_part[:, 0:PARTS, :], -1.0, None, ALU.mult)\
                .then_inc(s_bnp, 1)
            edge_terms(range(0, 9))
            dve.wait_ge(s_rows, 16 * TB)
            link(dve.tensor_copy(rows_f[0:TR, :, :], rows_i[0:TR, :, :]))
            for k in range(TB):
                ins = dve.tensor_scalar(below[0:TR, k, :], rows_f[0:TR, k, :], node0[0:TR, k:k + 1],
                                        None, ALU.is_lt, ALU.add, accum_out=nin[0:TR, k:k + 1])
            link(ins)
            link(dve.scalar_tensor_tensor(out=start_f[0:TR, :], in0=row_f[0:TR, :],
                                          scalar=float(FIRST_COLS), in1=nin[0:TR, :],
                                          op0=ALU.mult, op1=ALU.add))
            link(dve.tensor_copy(start_i[0:TR, :], start_f[0:TR, :]))
            link(dve.tensor_scalar(start_s[0:TR, :], start_i[0:TR, :], 4, None, ALU.arith_shift_right))
            link(dve.tensor_copy(start_sf[0:TR, :], start_s[0:TR, :]))
            link(dve.tensor_scalar(late[0:TR, :], start_f[0:TR, :], float(LATE), None, ALU.is_ge))
            link(dve.scalar_tensor_tensor(out=win_f[0:TR, :], in0=start_sf[0:TR, :],
                                          scalar=float(WROWS - 2), in1=late[0:TR, :],
                                          op0=ALU.min, op1=ALU.add))
            dve.tensor_copy(win_i[0:TR, :], win_f[0:TR, :]).then_inc(s_winidx, 1)
            edge_terms(range(9, 15))
            dve.wait_ge(s_win, 16 * TB)
            for k in range(TB):
                ins = dve.tensor_scalar(dr[0:TR, k, :], dsw[0:TR, k, 0:P], node0[0:TR, k:k + 1], None,
                                        ALU.subtract)
            steps[0] += 1
            ins.then_inc(dve_step, 1)
            dve.wait_ge(dve_step, steps[0])
            dve.tensor_scalar(away[0:TR, :, :], dr[0:TR, :, :], 0.0, float(FAR), ALU.is_lt, ALU.mult)\
                .then_inc(s_dr, 1)
            link(dve.tensor_scalar(far[0:TR, :, :], dr[0:TR, :, :], float(P), float(FAR), ALU.is_ge,
                                   ALU.mult))
            link(dve.tensor_tensor(away[0:TR, :, :], away[0:TR, :, :], far[0:TR, :, :], ALU.add))
            dve.tensor_tensor(far[0:TR, :, :], away[0:TR, :, :], dsw[0:TR, :, P:2 * P], ALU.add)\
                .then_inc(s_srcm, 1)
            edge_terms(range(15, 18))
            dve.wait_ge(s_pe0, 7)
            dve.tensor_copy(drel[:, :], pS[:, 0:TILES]).then_inc(dve_step, 1)
            steps[0] += 1
            dve.tensor_copy(srcidx[:, 0:TILES], R[2][:, 0:TILES]).then_inc(s_srcidx, 1)
            def ones_and_scores(b, half, use, tiles):
                for k in tiles:
                    dve.tensor_scalar(F[:, half * BATCH + k, :], iota_bf[:, :], drel_cur[:, half, k:k + 1], None,
                                      ALU.is_equal).then_inc(s_F, 1)
                    if k % GROUP == 0:
                        wait(dve, s_gather[half][k // GROUP], use, 16 * GROUP, 16 * GROUP)
                    dve.tensor_tensor_reduce(
                        out=junk[:, k % JUNK, :], in0=G[:, half * BATCH + k, :], in1=u_bc[:, :],
                        scale=1.0, scalar=0.0, op0=ALU.mult, op1=ALU.add,
                        accum_out=score[:, k:k + 1]).then_inc(s_score, 1)

            edge_terms(range(18, NECH))
            dve.wait_ge(s_ea_rest, 16)
            link(dve.tensor_tensor_reduce(out=ea_rest[:, :], in0=ea_rest[:, :], in1=v_bc[0:EREST, :],
                                          scale=1.0, scalar=0.0, op0=ALU.mult, op1=ALU.add,
                                          accum_out=c_rest[:, 0:1]))
            dve.tensor_scalar(c_out[:, :], c_main[:, :], const_c[:, 0:1], None, ALU.add)\
                .then_inc(s_cready, 1)
            dve.tensor_scalar(c_rest[:, 1:2], c_rest[:, 0:1], const_c[0:EREST, 0:1], None, ALU.add)\
                .then_inc(s_cready, 1)
            link(dve.tensor_scalar(full[0:TR, 0, :], dr[0:TR, :, P - 1], float(P), None, ALU.is_lt))
            link(dve.scalar_tensor_tensor(out=full[0:TR, 1, :], in0=win_f[0:TR, :],
                                          scalar=float(WROWS - 1), in1=full[0:TR, 0, :],
                                          op0=ALU.is_lt, op1=ALU.mult))
            dve.tensor_reduce(wrong[0:TR, 0:1], full[0:TR, 1, :], AX.X, ALU.add).then_inc(dve_step, 1)
            steps[0] += 1
            dve.wait_ge(s_order, 32)
            dve.tensor_copy(orest_f[:, :], orest_i[:, :]).then_inc(dve_step, 1)
            steps[0] += 1
            link(dve.tensor_copy(order_f[:, :], order_i[:, :]))
            dve.tensor_tensor(vrest[:, 1:EREST], orest_f[:, 0:EREST - 1], orest_f[:, 1:EREST], ALU.is_gt)\
                .then_inc(dve_step, 1)
            steps[0] += 1
            link(dve.tensor_tensor(viol[:, :], order_f[:, 0:EC], order_f[:, 1:EC + 1], ALU.is_gt))
            dve.tensor_reduce(wrong[0:1, 2:3], vrest[:, 1:EREST], AX.X, ALU.add).then_inc(dve_step, 1)
            steps[0] += 1
            link(dve.tensor_reduce(wrong[:, 1:2], viol[:, :], AX.X, ALU.add))
            dve.tensor_copy(drel_cur[:, 0, :], drel[:, 0:BATCH]).then_inc(s_wrong, 1)
            dve.wait_ge(s_pe0, 8)
            link(dve.tensor_reduce(wrong1[:, :], R[3][0:1, 4:7], AX.X, ALU.add))
            dve.tensor_scalar(flag[:, :], wrong1[:, :], 1.0, None, ALU.min).then_inc(s_flag, 1)
            dve.wait_ge(s_flag, 1)

            dve.wait_ge(s_dwin2, 16)
            link(dve.tensor_tensor(cont[:, :, 1:P], dwin[:, :, 1:P], dwin[:, :, 0:P - 1], ALU.is_equal))
            dve.tensor_scalar(neg[:, :, :], cont[:, :, :], -1.0, BIG, ALU.add, ALU.mult).then_inc(s_masks, 1)
            def window(t, b, at, n=P):
                if isinstance(b, int):
                    return t[:, b, at:at + n]
                return t[:, bass.ds(b, 1), at:at + n].rearrange("p a e -> p (a e)")

            def backward(part):
                return part[:, ::-1]

            def softmax(b, steps_):
                def after(i):
                    wait(dve, s_soft, b, 8, i)

                if 0 in steps_:
                    wait(dve, s_scoreT, b, 1, 1)
                    dve.tensor_tensor(z[:, :], scoreT, window(cwin, b, 0), ALU.add).then_inc(s_soft, 1)
                    after(1)
                    dve.scalar_tensor_tensor(out=a[:, :], in0=z[:, :], scalar=SLOPE, in1=z[:, :],
                                                op0=ALU.mult, op1=ALU.max).then_inc(s_soft, 1)
                    after(2)
                if 1 in steps_:
                    wait(dve, s_masked, b, 2, 2)
                    dve.tensor_tensor_scan(runmax[:, :], neg_cur[:, 0:P], a[:, :], -BIG,
                                              ALU.add, ALU.max).then_inc(s_soft, 1)
                    after(3)
                    dve.tensor_tensor_scan(backward(segmax), backward(neg_cur[:, 1:P + 1]),
                                              backward(runmax), -BIG, ALU.add, ALU.max)\
                        .then_inc(s_soft, 1)
                    after(4)
                    dve.tensor_tensor(shifted[:, :], a[:, :], segmax[:, :], ALU.subtract)\
                        .then_inc(s_shift, 1)
                if 2 in steps_:
                    wait(dve, s_exp, b, 1, 1)
                    dve.tensor_tensor_scan(runsum[:, :], cont_cur[:, 0:P], w[:, :], 0.0,
                                              ALU.mult, ALU.add).then_inc(s_soft, 1)
                    after(5)
                    dve.tensor_tensor_scan(backward(segsum), backward(cont_cur[:, 1:P + 1]),
                                              backward(runsum), 0.0, ALU.mult, ALU.max)\
                        .then_inc(s_soft, 1)
                    after(6)
                    dve.tensor_scalar(denom[:, :], segsum[:, :], 1e-16, None, ALU.add)\
                        .then_inc(s_soft, 1)
                    after(7)
                    dve.reciprocal(rdenom[:, :], denom[:, :]).then_inc(s_soft, 1)
                    after(8)
                    dve.tensor_tensor(alpha[:, :], w[:, :], rdenom[:, :], ALU.mult).then_inc(s_alpha, 1)

            def columns(b, half):
                wait(dve, s_alphaT, b, 1, 1)
                dve.tensor_copy(alpha_cur[:, half, :], alphaT).then_inc(s_ready, 1)

            def iteration(b, half, use):
                first, last = isinstance(b, int) and b == 0, isinstance(b, int) and b == NBATCH - 1
                tiles = LAST_USED if last else BATCH
                if not last:
                    if isinstance(b, int):
                        cols = drel[:, (b + 1) * BATCH:(b + 2) * BATCH]
                    else:
                        cols = drel[:, bass.ds((b + 1) * BATCH, BATCH)]
                    dve.tensor_copy(drel_cur[:, 1 - half, :], cols).then_inc(s_drel, 1)
                for j in range(BATCH + LAG_OFFSET if last else BATCH):
                    if not last:
                        if j == 0:
                            wait(dve, s_drel, b, 1, 1)
                        if j == SCORES_END + 6:
                            columns(b + 1, 1 - half)
                        ones_and_scores(b + 1, 1 - half, use + half, scored(j))
                        if j == SCORES_END + 1:
                            softmax(b + 1, (0,))
                        if j == SCORES_END + 2:
                            softmax(b + 1, (1,))
                        if j == SCORES_END + 4:
                            softmax(b + 1, (2,))
                    if (j >= 1 or not first) and (j - 1 < tiles or not last):
                        t = (j - 1) % BATCH
                        wait(dve, s_proj, b, BATCH, j)
                        if t % GROUP == 0 and j >= 1:
                            g = t // GROUP
                            wait(dve, s_xin[g], b, 16, 32 if last and g == GROUPS - 1 else 16)
                        tile = X[:, t // GROUP, t % GROUP, :]
                        dve.scalar_tensor_tensor(out=tile, in0=projected(t), scalar=0.0, in1=tile,
                                                 op0=ALU.max, op1=ALU.add).then_inc(s_y, 1)
                    g = (j - LAG_VAR) // GROUP
                    n, cols = group_columns(last, g)
                    if (j - LAG_VAR) % GROUP == 0 and (g >= 0 or not first) and g < GROUPS:
                        wait(dve, s_mv, b, BATCH, g * GROUP + n)
                        dve.tensor_scalar(var_e[:, cols], mv[:, cols, 1], EPS, None, ALU.add)\
                            .then_inc(s_var, 1)
                    g = (j - LAG_OFFSET) // GROUP
                    n, cols = group_columns(last, g)
                    if (j - LAG_OFFSET) % GROUP == 0 and (g >= 0 or not first) and g < GROUPS:
                        wait(dve, s_rstd, b, GROUPS, g + 1)
                        dve.scalar_tensor_tensor(out=nmr[:, cols], in0=mv[:, cols, 0], scalar=-1.0,
                                                 in1=rstd[:, cols], op0=ALU.mult, op1=ALU.mult)\
                            .then_inc(s_offset, 1)
                    if (j >= 2 or not first) and (j - 2 < tiles or not last):
                        t = (j - 2) % BATCH
                        wait(dve, s_y, b, BATCH, j - 1)
                        if not isinstance(b, int):
                            wait(dve, s_stats, b, BATCH, j - 2)
                        dve.bn_stats(stats[:, t % 4, :], X[:, t // GROUP, t % GROUP, :])\
                            .then_inc(s_stats, 1)
                    if (j >= 3 or not first) and (j - 3 < tiles or not last):
                        t = (j - 3) % BATCH
                        if isinstance(b, int):
                            wait(dve, s_stats, b, BATCH, j - 2)
                        dve.bn_aggr(mv[:, t, :], stats[:, t % 4, :]).then_inc(s_mv, 1)

            with dve.If(windows_fit(dve)):
                for k in range(BATCH):
                    if k >= JUNK:
                        dve.wait_ge(s_score, k - JUNK + 1)
                    ones_and_scores(0, 0, 0, [k])
                dve.wait_ge(s_cwin2, 16)
                softmax(0, (0, 1, 2))
                columns(0, 0)
                batches(dve, iteration)
            with dve.Else():
                dve.wait_ge(s_cwin2, 16)
                dve.wait_ge(s_clear, 5)
                dve.tensor_copy(bn_bc, A[0][:, 0:D]).then_inc(s_clear, 1)
                dve.tensor_scalar(earlier, iota_f[:, :], float(P), node0[:, 0:1], ALU.mult, ALU.is_lt)\
                    .then_inc(s_clear, 1)

                def match(step, n):
                    step(lambda: dve.tensor_scalar(same[0:n, 0:n], A[0][0:n, 0:n], dst_f[0:n, :], None,
                                                   ALU.is_equal))
                    step(lambda: dve.tensor_tensor_reduce(
                        out=penalty[0:n, 0:n], in0=same[0:n, 0:n], in1=earlier[0:n, 0:n], scale=1.0,
                        scalar=0.0, op0=ALU.mult, op1=ALU.add, accum_out=count_c[0:n, :]))
                    step(lambda: dve.tensor_scalar(taken_c[0:n, :], count_c[0:n, :], 0.0, float(FAR),
                                                   ALU.is_gt, ALU.mult))
                    step(lambda: dve.tensor_tensor(to_c[0:n, :], taken_c[0:n, :], dst_f[0:n, :], ALU.add))
                    step(lambda: dve.tensor_copy(to_i[0:n, :], to_c[0:n, :]))

                def maxima_tile(t, n):
                    wait_apart(dve, s_max_rows, t, MAXIMA_ROWS, MAXIMA_GATHERED)
                    step = tile_steps(dve, s_maxima, MAXIMA, t, "score")
                    step(lambda: dve.tensor_copy(dst_f[0:n, :], dst_i[0:n, :]))
                    step(lambda: dve.tensor_tensor_reduce(
                        out=y[0:n, :], in0=gx[0:n, 0:D], in1=u_bc[0:n, :], scale=1.0, scalar=0.0,
                        op0=ALU.mult, op1=ALU.add, accum_out=score_c[0:n, :]))
                    step(lambda: dve.tensor_tensor(z_c[0:n, :], score_c[0:n, :], term_c[0:n, :], ALU.add))
                    step(lambda: dve.scalar_tensor_tensor(out=a_c[0:n, :], in0=z_c[0:n, :], scalar=SLOPE,
                                                          in1=z_c[0:n, :], op0=ALU.mult, op1=ALU.max))
                    step(lambda: dve.tensor_scalar(diag[0:n, 0:n], ident[0:n, 0:n], dst_f[0:n, :], None,
                                                   ALU.mult))
                    step(lambda: dve.tensor_scalar(diag[0:n, n:2 * n], ident[0:n, 0:n], a_c[0:n, :], None,
                                                   ALU.mult))
                    step = tile_steps(dve, s_maxima, MAXIMA, t, "maximum")
                    match(step, n)
                    step(lambda: dve.tensor_tensor(masked[0:n, 0:n], A[0][0:n, n:2 * n], same[0:n, 0:n],
                                                   ALU.mult))
                    step(lambda: dve.tensor_scalar(penalty[0:n, 0:n], same[0:n, 0:n], -1.0, BIG, ALU.add,
                                                   ALU.mult))
                    step(lambda: dve.tensor_tensor(masked[0:n, 0:n], masked[0:n, 0:n], penalty[0:n, 0:n],
                                                   ALU.add))
                    step(lambda: dve.tensor_reduce(max_loc[0:n, :], masked[0:n, 0:n], AX.X, ALU.max))
                    step(lambda: dve.tensor_tensor(max_new[0:n, :], max_loc[0:n, :], max_old[0:n, :],
                                                   ALU.max))

                def sums_tile(t, n):
                    wait_apart(dve, s_sum_rows, t, SUMS_ROWS, SUMS_GATHERED)
                    step = tile_steps(dve, s_sums, SUMS, t, "shift")
                    step(lambda: dve.tensor_copy(dst_f[0:n, :], dst_i[0:n, :]))
                    step(lambda: dve.tensor_scalar(diag[0:n, 0:n], ident[0:n, 0:n], dst_f[0:n, :], None,
                                                   ALU.mult))
                    step(lambda: dve.tensor_tensor(shift_c[0:n, :], a_c[0:n, :], max_old[0:n, :],
                                                   ALU.subtract))
                    step = tile_steps(dve, s_sums, SUMS, t, "match")
                    match(step, n)
                    step(lambda: dve.tensor_scalar(masked[0:n, 0:n], same[0:n, 0:n], w_c[0:n, :], None,
                                                   ALU.mult))
                    step = tile_steps(dve, s_sums, SUMS, t, "add")
                    step(lambda: dve.tensor_tensor(new[0:n, :], A[1][0:n, 0:D + 1], old[0:n, :], ALU.add))

                def nodes_tile(t, n):
                    step = tile_steps(dve, s_nodes, NODES, t, "divide")
                    weight = old[0:n, D:D + 1]
                    step(lambda: dve.tensor_scalar(den_c[0:n, :], weight, 1e-16, None, ALU.add))
                    step(lambda: dve.reciprocal(rden_c[0:n, :], den_c[0:n, :]))
                    step(lambda: dve.tensor_tensor(has_c[0:n, :], weight, rden_c[0:n, :], ALU.mult))
                    step(lambda: dve.tensor_scalar(new[0:n, 0:D], old[0:n, 0:D], rden_c[0:n, :], None,
                                                   ALU.mult))
                    step(lambda: dve.tensor_scalar(bias[0:n, :], bn_bc[0:n, :], has_c[0:n, :], None,
                                                   ALU.mult))
                    step = tile_steps(dve, s_nodes, NODES, t, "copy")
                    step(lambda: dve.tensor_copy(
                        AT[:, 0, :, 0:n],
                        R[0][:, 0:D].rearrange("p (c n) -> p c n", c=KC)[:, :, 0:n]))
                    step = tile_steps(dve, s_nodes, NODES, t, "norm")
                    step(lambda: dve.tensor_tensor(y[0:n, :], R[1][0:n, 0:D], bias[0:n, :], ALU.add))
                    step(lambda: dve.scalar_tensor_tensor(out=y[0:n, :], in0=y[0:n, :], scalar=0.0,
                                                          in1=xrow[0:n, :], op0=ALU.max, op1=ALU.add))
                    step(lambda: dve.bn_stats(stats_c[0:n, :], y[0:n, :]))
                    step(lambda: dve.bn_aggr(mv_c[0:n, :], stats_c[0:n, :]))
                    step(lambda: dve.tensor_scalar(var_c[0:n, :], mv_c[0:n, 1:2], EPS, None, ALU.add))
                    step = tile_steps(dve, s_nodes, NODES, t, "apply")
                    step(lambda: dve.tensor_scalar(y[0:n, :], y[0:n, :], mv_c[0:n, 0:1], rstd_c[0:n, :],
                                                   ALU.subtract, ALU.mult))

                edge_tiles(dve, maxima_tile)
                edge_tiles(dve, sums_tile)
                node_tiles(dve, nodes_tile)


_INS = ["x", "src", "dst", "edge_attr_128", "L0_gnn_Wn", "L0_gnn_bn", "L0_gnn_We", "L0_gnn_be", "L0_gnn_attn"]


def kernel(**inputs):
    import concourse.bacc as bacc
    from concourse.bass_utils import run_bass_kernel_spmd

    nc = bacc.Bacc("TRN2", target_bir_lowering=False, num_devices=1)
    arrays, args = {}, []
    for name in _INS:
        array = np.ascontiguousarray(inputs[name])
        arrays[f"in_{name}"] = array
        args.append(nc.dram_tensor(f"in_{name}", array.shape, mybir.dt.from_np(array.dtype),
                                   kind="ExternalInput").ap())
    out = nc.dram_tensor("out", (N, D), F32, kind="ExternalOutput").ap()
    gnn_kernel(nc, *args, out)
    result = run_bass_kernel_spmd(nc, [arrays], core_ids=[0])
    return result.results[0]["out"]
```

```python
from contextlib import ExitStack

import numpy as np

import concourse.bass as bass
from concourse import mybir
from concourse.alu_op_type import AluOpType as ALU

F32 = mybir.dt.float32
BF16 = mybir.dt.bfloat16
I32 = mybir.dt.int32
ACT = mybir.ActivationFunctionType
AX = mybir.AxisListType

P = 128
N, D = 50000, 256
E, KE = 25000, 128
KC = D // P
SLOPE = 0.01
EPS = 1e-5
BATCH, GROUP = 28, 4
NBATCH = 14
GROUPS = BATCH // GROUP
TILES = BATCH * NBATCH
LAST_TILE = N // P
LAST_ROWS = N - LAST_TILE * P
LAST_USED = LAST_TILE - (NBATCH - 1) * BATCH + 1
FIRST_COLS = 200
FIRST_ROWS = E // FIRST_COLS
TB, TR = 4, 98
STEP = 16
WROWS = (E - P) // STEP + 2
WMAIN = (WROWS - 1) // 16 * 16
LATE = E - P
FAR = 1 << 20
BIG = 3.0e38
EC = E // P
EREST = E - EC * P
ECH = 5
NECH = EC // ECH
EPE = 2
ERING = 6
SCORED = [2, 2, 1, 1] * 4 + [1] * 4
MASKS_SLOT, TURN_SLOT, SOFT0, SOFT1, EXP_SLOT, SOFT2, ALPHA_SLOT, COLUMNS = 16, 20, 21, 22, 23, 24, 26, 27
LEAD = 2
LAG_VAR, LAG_POW, LAG_OFFSET = 7, 8, 14
LAG_APPLY = 15
PARTS = 3
FIRST_POWERS = (2, 6, 11, 16, 21)
JUNK = 6
ZERO_STEPS = 14
ZERO_BLOCKS = 2 * BATCH * KC // ZERO_STEPS
WT_AT, DWIN_AT, TURN_AT, SRC_AT = 6, 16, 12, 13
CHECK_AT, SCORES_AT, FLAG_AT, WEIGHTS_AT = 22, 29, 27, 2
CW_AT = 8

assert TB * TR == TILES and sum(SCORED) == BATCH and NECH * ECH == EC and LATE % 8 == 0


def stages(*parts):
    at, found = 1, {}
    for name, adds in parts:
        found[name] = at
        at += adds
    found["all"] = at - 1
    return found


MAXIMA = stages(("load", 48), ("gather", 0), ("score", 6), ("spread", 1), ("maximum", 10), ("save", 16))
SUMS = stages(("load", 48), ("gather", 0), ("shift", 3), ("spread", 2), ("match", 6), ("sum", 1),
              ("add", 1), ("save", 0))
MAXIMA_GATHERED, MAXIMA_ROWS = 32, 48
SUMS_GATHERED, SUMS_ROWS = 48, 64
NODES = stages(("load", 32), ("divide", 5), ("turn", 1), ("copy", 1), ("project", 1), ("norm", 5),
               ("root", 1), ("apply", 1), ("save", 16))
NROWS = (N + P - 1) // P * P
EDGE_TILES = E // P


def starts(j):
    return sum(SCORED[:j])


def scored(j):
    return range(starts(j), starts(j + 1)) if 0 <= j < len(SCORED) else ()


def gnn_kernel(nc, x, src, dst, edge, Wn, bn, We, be, attn, out):
    with ExitStack() as ctx:
        def sb(name, shape, dt=F32):
            return ctx.enter_context(nc.sbuf_tensor(name, shape, dt))

        def ps(name, shape, dt=F32):
            return ctx.enter_context(nc.psum_tensor(name, shape, dt))

        def sem(name):
            return ctx.enter_context(nc.semaphore(name))

        def dram(name, shape, dt):
            return nc.dram_tensor(name, shape, dt, kind="Internal")

        ds_table = dram("ds_table", [WROWS, 2 * P], I32)
        c_table = dram("c_table", [WROWS, P], F32)
        c_lin = dram("c_lin", [1, E], F32)
        dwin_dram = dram("dwin_dram", [TILES, P], F32)
        cwin_dram = dram("cwin_dram", [TILES, P], F32)

        max_dram = dram("max_dram", [NROWS, 1], F32)
        sum_dram = dram("sum_dram", [NROWS, D + 1], F32)
        a_lin = dram("a_lin", [E, 1], F32)

        ident = sb("ident", [P, P])
        ones_row = sb("ones_row", [1, P])
        ones_col = sb("ones_col", [P, 1])
        ones_bf = sb("ones_bf", [P, P], BF16)
        ones_sq = sb("ones_sq", [P, P])
        iota_i = sb("iota_i", [P, P], I32)
        iota_f = sb("iota_f", [P, P])
        iota_bf = sb("iota_bf", [P, P], BF16)
        node0_i = sb("node0_i", [P, TB], I32)
        node0 = sb("node0", [P, TB])
        power = sb("power", [P, GROUP])
        u_bc = sb("u_bc", [P, D])
        v_bc = sb("v_bc", [P, KE])
        v_col = sb("v_col", [P, 1])
        const_c = sb("const_c", [P, 1])
        WT = sb("WT", [P, KC, D])
        bn6 = sb("bn6", [2 * PARTS, D], BF16)
        pick6 = sb("pick6", [P, 2 * PARTS], BF16)

        Wn_sb = sb("Wn_sb", [P, KC, D])
        We_sb = sb("We_sb", [P, KC, KE])
        attn_c = sb("attn_c", [P, KC])
        attn_rep = sb("attn_rep", [P, KC, P])
        bn_c = sb("bn_c", [P, KC])
        be_c = sb("be_c", [P, KC])
        bne = sb("bne", [P, KC])
        bn_row = sb("bn_row", [1, D])
        bn_rest = sb("bn_rest", [1, 2, D])
        bn_part = sb("bn_part", [1, 2 * PARTS, D], BF16)
        firsts_i = sb("firsts_i", [1, FIRST_ROWS], I32)
        firsts = sb("firsts", [1, FIRST_ROWS])
        below = sb("below", [P, TB, FIRST_COLS], BF16)
        nrows = sb("nrows", [P, TB])
        row_f = sb("row_f", [P, TB])
        row_i = sb("row_i", [P, TB], I32)
        rows_i = sb("rows_i", [P, TB, FIRST_COLS], I32)
        rows_f = sb("rows_f", [P, TB, FIRST_COLS])
        nin = sb("nin", [P, TB])
        start_f = sb("start_f", [P, TB])
        start_i = sb("start_i", [P, TB], I32)
        start_s = sb("start_s", [P, TB], I32)
        start_sf = sb("start_sf", [P, TB])
        late = sb("late", [P, TB])
        win_f = sb("win_f", [P, TB])
        win_i = sb("win_i", [P, TB], I32)
        dsw = sb("dsw", [P, TB, 2 * P], I32)
        dr = sb("dr", [P, TB, P])
        away = sb("away", [P, TB, P])
        far = sb("far", [P, TB, P])
        cw = sb("cw", [P, TB, P])
        order_i = sb("order_i", [P, EC + 1], I32)
        order_f = sb("order_f", [P, EC + 1])
        orest_i = sb("orest_i", [1, EREST], I32)
        orest_f = sb("orest_f", [1, EREST])
        viol = sb("viol", [P, EC])
        vrest = sb("vrest", [1, EREST])
        full = sb("full", [P, 2, TB])
        wrong = sb("wrong", [P, 3])
        wrong1 = sb("wrong1", [1, 1])
        flag = sb("flag", [1, 1], I32)
        ea = sb("ea", [P, ERING, ECH, KE])
        ea_rest = sb("ea_rest", [EREST, KE])
        c_main = sb("c_main", [P, EC])
        c_out = sb("c_out", [P, EC])
        c_rest = sb("c_rest", [EREST, 2])

        drel = sb("drel", [P, TILES])
        srcidx = sb("srcidx", [P, TILES + BATCH], I32)
        dwin = sb("dwin", [BATCH, NBATCH, P])
        cwin = sb("cwin", [BATCH, NBATCH, P])
        idx_cur = sb("idx_cur", [P, 2, BATCH], I32)
        drel_cur = sb("drel_cur", [P, 2, BATCH])
        alpha_cur = sb("alpha_cur", [P, 2, BATCH])
        cont = sb("cont", [BATCH, P + 1])
        neg = sb("neg", [BATCH, P + 1])
        score = sb("score", [P, BATCH])
        z = sb("z", [BATCH, P])
        a = sb("a", [BATCH, P])
        runmax = sb("runmax", [BATCH, P])
        segmax = sb("segmax", [BATCH, P])
        shifted = sb("shifted", [BATCH, P])
        w = sb("w", [BATCH, P])
        runsum = sb("runsum", [BATCH, P])
        segsum = sb("segsum", [BATCH, P])
        denom = sb("denom", [BATCH, P])
        rdenom = sb("rdenom", [BATCH, P])
        alpha = sb("alpha", [BATCH, P])

        G = sb("G", [P, 2 * BATCH, D])
        M = sb("M", [P, 4, P])
        F = sb("F", [P, 2 * BATCH, P], BF16)
        bias_on = sb("bias_on", [2 * PARTS, 2, GROUP * P], BF16)
        junk = sb("junk", [P, JUNK, D], BF16)
        AT = sb("AT", [P, 2, KC, P])
        X = sb("X", [P, GROUPS, GROUP, D])
        stats = sb("stats", [P, 4, 6])
        mv = sb("mv", [P, BATCH, 2])
        var_e = sb("var_e", [P, BATCH])
        rstd = sb("rstd", [P, BATCH])
        nmr = sb("nmr", [P, BATCH])

        G_flat = G[:, :, :].rearrange("p a d -> p (a d)")

        def part_of_G(at, n):
            return G_flat[:, at * D:at * D + n]

        gx, old, new = part_of_G(0, D + 1), part_of_G(2, D + 1), part_of_G(4, D + 1)
        same, masked, penalty = part_of_G(6, P), part_of_G(7, P), part_of_G(8, P)
        earlier, least, nothing = part_of_G(9, P), part_of_G(10, NROWS // P), part_of_G(12, D + 1)
        diag, bn_bc, bias = part_of_G(14, 2 * P), part_of_G(15, D), part_of_G(16, D)
        y, xrow = part_of_G(17, D), part_of_G(18, D)
        cols = part_of_G(19, 32)
        (dst_f, score_c, term_c, z_c, a_c, max_old, max_loc, max_new, count_c, taken_c, to_c, shift_c,
         w_c, den_c, rden_c, has_c, var_c, rstd_c) = (cols[:, i:i + 1] for i in range(18))
        mv_c, stats_c = cols[:, 20:22], cols[:, 24:30]
        icols = sb("icols", [P, 3], I32)
        src_i, dst_i, to_i = (icols[:, i:i + 1] for i in range(3))

        def turned_edges(c):
            return X[:, 0, (c % 2) * 2:(c % 2) * 2 + 2, :].rearrange("p a d -> p (a d)")[:, 0:EPE * P]

        A = [ps(f"A{i}", [P, 512]) for i in range(2)]
        R = [ps(f"R{i}", [P, 512]) for i in range(4)]
        pS = ps("pS", [P, 512])
        pC = ps("pC", [P, 512])
        scoreT, alphaT, edges6 = pS[0:BATCH, 0:P], pS[:, P:P + BATCH], pC[0:2 * PARTS, :]

        turning = [pC, A[0]]
        pe_terms = R[1][:, 0:NECH * EPE]

        def projected(j):
            return R[j % 4][:, 0:D]

        s_const = sem("s_const")
        s_iota = sem("s_iota")
        s_vload = sem("s_vload")
        s_wload = sem("s_wload")
        s_first = sem("s_first")
        s_order = sem("s_order")
        s_dst_tab = sem("s_dst_tab")
        s_rows = sem("s_rows")
        s_win = sem("s_win")
        s_dwin = sem("s_dwin")
        s_dwin2 = sem("s_dwin2")
        s_ea = [sem(f"s_ea{i}") for i in range(ERING)]
        s_ea_rest = sem("s_ea_rest")
        s_cstore = sem("s_cstore")
        s_ctab = sem("s_ctab")
        s_cw = sem("s_cw")
        s_cwin0 = sem("s_cwin0")
        s_cwin = sem("s_cwin")
        s_cwin2 = sem("s_cwin2")
        s_bn6 = sem("s_bn6")
        dve_step = sem("dve_step")
        s_pe0 = sem("s_pe0")
        s_attn = sem("s_attn")
        s_rowidx = sem("s_rowidx")
        s_winidx = sem("s_winidx")
        s_dr = sem("s_dr")
        s_srcm = sem("s_srcm")
        s_srcidx = sem("s_srcidx")
        s_bnp = sem("s_bnp")
        s_wrong = sem("s_wrong")
        s_flag = sem("s_flag")
        s_ttr = sem("s_ttr")
        s_v = sem("s_v")
        s_turn = sem("s_turn")
        s_turned = sem("s_turned")
        s_edot = sem("s_edot")
        s_cready = sem("s_cready")
        s_gzero = sem("s_gzero")
        s_WT = sem("s_WT")
        s_idx = sem("s_idx")
        s_gather = [[sem(f"s_gather{h}_{g}") for g in range(GROUPS)] for h in range(2)]
        s_drel = sem("s_drel")
        s_F = sem("s_F")
        s_score = sem("s_score")
        s_edges = sem("s_edges")
        s_bias = sem("s_bias")
        s_scoreT = sem("s_scoreT")
        s_soft = sem("s_soft")
        s_shift = sem("s_shift")
        s_exp = sem("s_exp")
        s_alpha = sem("s_alpha")
        s_alphaT = sem("s_alphaT")
        s_ready = sem("s_ready")
        s_M = sem("s_M")
        s_agg = sem("s_agg")
        s_AT = sem("s_AT")
        s_proj = sem("s_proj")
        s_y = sem("s_y")
        s_stats = sem("s_stats")
        s_mv = sem("s_mv")
        s_var = sem("s_var")
        s_rstd = sem("s_rstd")
        s_offset = sem("s_offset")
        s_apply = sem("s_apply")
        s_xin = [sem(f"s_xin{g}") for g in range(GROUPS)]
        s_xout = [sem(f"s_xout{g}") for g in range(GROUPS)]

        s_clear = sem("s_clear")
        s_maxima = sem("s_maxima")
        s_sums = sem("s_sums")
        s_nodes = sem("s_nodes")
        s_max_rows = sem("s_max_rows")
        s_sum_rows = sem("s_sum_rows")
        CLEAR_SETUP = 7
        CLEARED = CLEAR_SETUP + 16 * (NROWS // P + 1)

        def wait(eng, s, batch, per, extra=0):
            if isinstance(batch, int) and batch * per + extra <= 0:
                return
            eng.wait_ge(s, batch * per + extra)

        def wait_apart(eng, s, batch, per, extra=0):
            if isinstance(batch, int):
                wait(eng, s, batch, per, extra)
                return
            value = eng.to_reg(batch * per + extra)
            eng.wait_ge(s_const, 1)
            eng.wait_ge(s, value)

        def tile_stage(eng, s, plan, t, stage, beyond=0):
            wait_apart(eng, s, t, plan["all"], plan[stage] + beyond)

        def tile_steps(eng, s, plan, t, stage):
            n = [0]

            def step(make):
                tile_stage(eng, s, plan, t, stage, n[0])
                n[0] += 1
                make().then_inc(s, 1)
            return step

        def edge_tiles(eng, tile):
            with eng.Fori(0, EDGE_TILES) as t:
                tile(t, P)
            tile(EDGE_TILES, EREST)

        def node_tiles(eng, tile):
            with eng.Fori(0, LAST_TILE) as t:
                tile(t, P)
            tile(LAST_TILE, LAST_ROWS)

        def rows_at(tensor, t, n):
            return tensor[t * P:t * P + n, :] if isinstance(t, int) else tensor[bass.ds(t * P, n), :]

        def windows_fit(eng):
            eng.wait_ge(s_flag, 1)
            return eng.value_load(flag[0:1, 0:1], min_val=0, max_val=1) == 0

        def batches(eng, iteration):
            iteration(0, 0, 0)
            with eng.Fori(0, NBATCH // 2 - 1) as q:
                iteration(q * 2 + 1, 1, q)
                iteration(q * 2 + 2, 0, q + 1)
            iteration(NBATCH - 1, 1, NBATCH // 2 - 1)

        def group_columns(last, g):
            n = LAST_USED % GROUP if last and g == GROUPS - 1 else GROUP
            at = g % GROUPS * GROUP
            return n, slice(at, at + n)

        def windows_of(tensor):
            t, o = tensor.tensor, tensor.offset
            return [
                (slice(0, WMAIN), bass.AP(tensor=t, offset=o, ap=[[STEP, WMAIN], [1, P]])),
                (slice(WMAIN, WROWS - 1),
                 bass.AP(tensor=t, offset=o + STEP * WMAIN, ap=[[STEP, WROWS - 1 - WMAIN], [1, P]])),
                (slice(WROWS - 1, WROWS), bass.AP(tensor=t, offset=o + LATE, ap=[[P, 1], [1, P]])),
            ]

        def group_rows(tensor, b, g):
            row = (b * BATCH + g * GROUP) * P
            if isinstance(row, int):
                part = tensor[row:row + GROUP * P, :]
            else:
                part = tensor[bass.ds(row, GROUP * P), :]
            return part.rearrange("(a p) d -> p a d", p=P)

        block = ctx.enter_context(nc.Block())

        @block.sync
        def _(sp):
            sp.dma_start(firsts_i[:, :], dst.rearrange("(a r c) -> a r c", a=1, c=FIRST_COLS)[:, :, 0],
                         allow_slow_non_contiguous=True).then_inc(s_first, 16)
            sp.dma_start(attn_c[:, :], attn.rearrange("a h (c p) -> p (a h c)", p=P),
                         allow_slow_non_contiguous=True).then_inc(s_vload, 16)
            sp.dma_start(We_sb[:, :, :], We.rearrange("(c p) k -> p c k", p=P)).then_inc(s_vload, 16)
            main = edge[0:EC * P, :].rearrange("(p e) k -> p e k", e=EC)

            def load_edges(c):
                if c >= ERING:
                    sp.wait_ge(s_ttr, c - ERING + 1)
                    sp.wait_ge(s_turn, c - ERING + 1)
                sp.dma_start(ea[:, c % ERING, :, :], main[:, c * ECH:(c + 1) * ECH, :])\
                    .then_inc(s_ea[c % ERING], 16)

            for c in range(WEIGHTS_AT):
                load_edges(c)
            sp.dma_start(bn_c[:, :], bn.rearrange("(c p) -> p c", p=P),
                         allow_slow_non_contiguous=True).then_inc(s_wload, 16)
            sp.dma_start(be_c[:, :], be.rearrange("(c p) -> p c", p=P),
                         allow_slow_non_contiguous=True).then_inc(s_wload, 16)
            sp.dma_start(bn_row[:, :], bn.rearrange("(a d) -> a d", a=1)).then_inc(s_wload, 16)
            sp.dma_start(Wn_sb[:, :, :], Wn.rearrange("(c p) k -> p c k", p=P)).then_inc(s_wload, 16)
            for c in range(WEIGHTS_AT, NECH):
                if c == ERING:
                    sp.dma_start(ea_rest[:, :], edge[EC * P:E, :]).then_inc(s_ea_rest, 16)
                    t, o = dst.tensor, dst.offset
                    sp.dma_start(order_i[:, :], bass.AP(tensor=t, offset=o, ap=[[EC, P], [1, EC + 1]]))\
                        .then_inc(s_order, 16)
                    sp.dma_start(orest_i[:, :], dst.rearrange("(a e) -> a e", a=1)[:, EC * P:E])\
                        .then_inc(s_order, 16)
                load_edges(c)
            sp.wait_ge(s_bnp, 1)
            for i in range(2 * PARTS):
                sp.dma_start(bn6[i:i + 1, :], bn_part[:, i, :]).then_inc(s_bn6, 16)
            for g in range(GROUPS):
                if g == 0:
                    sp.wait_ge(s_cwin0, 16)
                if g == 3:
                    sp.wait_ge(s_cw, 16 * TB)
                    sp.dma_start(cwin_dram[:, :].rearrange("(k p) e -> p k e", p=TR), cw[0:TR, :, :])\
                        .then_inc(s_cwin, 16)
                if g == 4:
                    sp.wait_ge(s_cwin, 16)
                    sp.dma_start(cwin[:, 1:NBATCH, :],
                                 cwin_dram[BATCH:TILES, :].rearrange("(b p) e -> p b e", p=BATCH))\
                        .then_inc(s_cwin2, 16)
                sp.dma_start(X[:, g, :, :], group_rows(x, 0, g)).then_inc(s_xin[g], 16)

            def load(b, g, known_last):
                if known_last and g == GROUPS - 1:
                    full_rows = (LAST_TILE % GROUP) * P
                    row = (LAST_TILE - LAST_TILE % GROUP) * P
                    sp.dma_start(X[:, g, 0:LAST_TILE % GROUP, :],
                                 x[row:row + full_rows, :].rearrange("(a p) d -> p a d", p=P))\
                        .then_inc(s_xin[g], 16)
                    sp.dma_start(X[0:LAST_ROWS, g, LAST_TILE % GROUP, :], x[LAST_TILE * P:N, :])\
                        .then_inc(s_xin[g], 16)
                else:
                    sp.dma_start(X[:, g, :, :], group_rows(x, b, g)).then_inc(s_xin[g], 16)

            def iteration(b, half, use):
                first, last = isinstance(b, int) and b == 0, isinstance(b, int) and b == NBATCH - 1
                for g in range(GROUPS):
                    short = last and g == GROUPS - 1
                    wait(sp, s_apply, b, BATCH, LAST_USED if short else g * GROUP + GROUP)
                    if short:
                        row = (LAST_TILE - LAST_TILE % GROUP) * P
                        sp.dma_start(out[row:LAST_TILE * P, :].rearrange("(a p) d -> p a d", p=P),
                                     X[:, g, 0:LAST_TILE % GROUP, :]).then_inc(s_xout[g], 16)
                        sp.dma_start(out[LAST_TILE * P:N, :], X[0:LAST_ROWS, g, LAST_TILE % GROUP, :])\
                            .then_inc(s_xout[g], 16)
                    else:
                        sp.dma_start(group_rows(out, b, g), X[:, g, :, :]).then_inc(s_xout[g], 16)
                    if g == 0 and not first:
                        wait(sp, s_xout[GROUPS - 1], b, 16)
                        load(b, GROUPS - 1, last)
                    if g >= 1 and not last:
                        wait(sp, s_xout[g - 1], b, 16, 16)
                        load(b + 1, g - 1, False)

            with sp.If(windows_fit(sp)):
                batches(sp, iteration)
                for g in range(GROUPS):
                    sp.wait_ge(s_xout[g], 16 * (NBATCH + (g == GROUPS - 1)))
            with sp.Else():
                sp.wait_ge(s_clear, CLEAR_SETUP)
                with sp.Fori(0, NROWS // P) as t:
                    sp.dma_start(sum_dram[bass.ds(t * P, P), :], nothing).then_inc(s_clear, 16)
                sp.dma_start(max_dram[:, :].rearrange("(p r) a -> p (r a)", p=P), least)\
                    .then_inc(s_clear, 16)
                sp.wait_ge(s_cstore, 32)
                sp.wait_ge(s_bn6, 16 * 2 * PARTS)
                for g in range(GROUPS):
                    sp.wait_ge(s_xin[g], 16)
                src_rows = src.rearrange("(e a) -> e a", a=1)
                dst_rows = dst.rearrange("(e a) -> e a", a=1)
                term_rows = c_lin[:, :].rearrange("a e -> e a")

                def load(s, t, n, third, into):
                    for rows, to in ((src_rows, src_i), (dst_rows, dst_i), (third, into)):
                        sp.dma_start(to[0:n, :], rows_at(rows, t, n), allow_slow_non_contiguous=True)\
                            .then_inc(s, 16)

                def maxima_tile(t, n):
                    tile_stage(sp, s_maxima, MAXIMA, t, "load")
                    load(s_maxima, t, n, term_rows, term_c)
                    tile_stage(sp, s_maxima, MAXIMA, t, "save")
                    sp.dma_start(rows_at(a_lin, t, n), a_c[0:n, :], allow_slow_non_contiguous=True)\
                        .then_inc(s_maxima, 16)

                def sums_tile(t, n):
                    tile_stage(sp, s_sums, SUMS, t, "load")
                    load(s_sums, t, n, a_lin, a_c)

                def nodes_tile(t, n):
                    tile_stage(sp, s_nodes, NODES, t, "load")
                    sp.dma_start(old[0:n, :], rows_at(sum_dram, t, n)).then_inc(s_nodes, 16)
                    sp.dma_start(xrow[0:n, :], rows_at(x, t, n)).then_inc(s_nodes, 16)
                    tile_stage(sp, s_nodes, NODES, t, "save")
                    sp.dma_start(rows_at(out, t, n), y[0:n, :]).then_inc(s_nodes, 16)

                edge_tiles(sp, maxima_tile)
                edge_tiles(sp, sums_tile)
                node_tiles(sp, nodes_tile)
                sp.wait_ge(s_nodes, NODES["all"] * (LAST_TILE + 1) + 1)

        @block.gpsimd
        def _(pool):
            pool.memset(ident[:, :], 0.0).then_inc(s_iota, 1)
            pool.iota(node0_i[:, :], [[TR * P, TB]], base=0, channel_multiplier=P).then_inc(s_const, 1)
            pool.iota(iota_i[:, :], [[1, P]], base=0, channel_multiplier=0).then_inc(s_const, 1)
            pool.memset(ones_row[:, :], 1.0).then_inc(s_const, 1)
            pool.memset(ones_col[:, :], 1.0).then_inc(s_const, 1)
            pool.memset(ones_bf[:, :], 1.0).then_inc(s_const, 1)
            pool.memset(ones_sq[:, :], 1.0).then_inc(s_const, 1)
            pool.memset(power[:, :], -0.5).then_inc(s_const, 1)
            pool.memset(pick6[:, 0:PARTS], 0.0).then_inc(s_const, 1)
            pool.memset(pick6[:, PARTS:2 * PARTS], 1.0).then_inc(s_const, 1)
            pool.memset(srcidx[:, TILES:TILES + BATCH], FAR).then_inc(s_const, 1)
            pool.wait_ge(s_iota, 1)
            pool.affine_select(out=ident[:, :], in_=ident[:, :], compare_op=ALU.not_equal, fill=1.0,
                               base=0, pattern=[[-1, P]], channel_multiplier=1).then_inc(s_const, 1)
            pool.wait_ge(s_rowidx, 1)
            for k in range(TB):
                pool.indirect_dma_start(
                    rows_i[0:TR, k, :], None, dst.rearrange("(r c) -> r c", c=FIRST_COLS),
                    bass.IndirectOffsetOnAxis(ap=row_i[0:TR, k:k + 1], axis=0),
                    bounds_check=FIRST_ROWS - 1, oob_is_err=False).then_inc(s_rows, 16)
            pool.wait_ge(s_winidx, 1)
            pool.wait_ge(s_dst_tab, 96)
            for k in range(TB):
                pool.indirect_dma_start(
                    dsw[0:TR, k, :], None, ds_table[:, :],
                    bass.IndirectOffsetOnAxis(ap=win_i[0:TR, k:k + 1], axis=0),
                    bounds_check=WROWS - 1, oob_is_err=False).then_inc(s_win, 16)
            pool.wait_ge(s_gzero, ZERO_STEPS)
            pool.wait_ge(s_srcidx, 1)

            def copy_indices(b, half):
                if isinstance(b, int):
                    cols = srcidx[:, b * BATCH:(b + 1) * BATCH]
                else:
                    cols = srcidx[:, bass.ds(b * BATCH, BATCH)]
                pool.tensor_copy(idx_cur[:, half, :], cols).then_inc(s_idx, 1)

            def gather(half, j):
                pool.indirect_dma_start(
                    G[:, half * BATCH + j, :], None, x,
                    bass.IndirectOffsetOnAxis(ap=idx_cur[:, half, j:j + 1], axis=0),
                    bounds_check=N - 1, oob_is_err=False).then_inc(s_gather[half][j // GROUP], 16)

            for b in range(2):
                copy_indices(b, b)
                pool.wait_ge(s_idx, b + 1)
                for j in range(BATCH):
                    if b == 1 and j == CW_AT:
                        pool.wait_ge(s_ctab, 48)
                        pool.indirect_dma_start(
                            cwin[:, 0, :], None, c_table[:, :],
                            bass.IndirectOffsetOnAxis(ap=win_i[0:BATCH, 0:1], axis=0),
                            bounds_check=WROWS - 1, oob_is_err=False).then_inc(s_cwin0, 16)
                        for k in range(TB):
                            pool.indirect_dma_start(
                                cw[0:TR, k, :], None, c_table[:, :],
                                bass.IndirectOffsetOnAxis(ap=win_i[0:TR, k:k + 1], axis=0),
                                bounds_check=WROWS - 1, oob_is_err=False).then_inc(s_cw, 16)
                    gather(b, j)

            def iteration(b, half, use):
                first, last = isinstance(b, int) and b == 0, isinstance(b, int) and b == NBATCH - 1
                for j in range(BATCH + LAG_POW if last else BATCH):
                    if not last:
                        wait_apart(pool, s_agg, b, BATCH, j + 1)
                        if j == 0:
                            copy_indices(b + 2, half)
                            wait_apart(pool, s_idx, b, 1, 3)
                        gather(half, j)
                    g = (j - LAG_POW) // GROUP
                    due = (j - LAG_POW) % GROUP == 0 and g < GROUPS
                    if first:
                        due = j in FIRST_POWERS
                        g = FIRST_POWERS.index(j) if due else 0
                    n, cols = group_columns(last, g)
                    if due:
                        wait(pool, s_var, b, GROUPS, g + 1)
                        pool.tensor_tensor(rstd[:, cols], var_e[:, cols], power[:, 0:n], ALU.pow)\
                            .then_inc(s_rstd, 1)

            with pool.If(windows_fit(pool)):
                batches(pool, iteration)
                for g in range(GROUPS):
                    pool.wait_ge(s_gather[0][g], 16 * GROUP * (NBATCH // 2 + 1))
                    pool.wait_ge(s_gather[1][g], 16 * GROUP * (NBATCH // 2))
            with pool.Else():
                pool.wait_ge(s_score, BATCH)
                for g in range(GROUPS):
                    pool.wait_ge(s_gather[0][g], 16 * GROUP)
                    pool.wait_ge(s_gather[1][g], 16 * GROUP)
                pool.memset(nothing, 0.0).then_inc(s_clear, 1)
                pool.memset(least, -BIG).then_inc(s_clear, 1)
                pool.memset(cols, 0.0).then_inc(s_clear, 1)
                pool.memset(gx[:, D:D + 1], 1.0).then_inc(s_clear, 1)

                def rows_of(s, to, table, index, n):
                    pool.indirect_dma_start(
                        to[0:n, :], None, table, bass.IndirectOffsetOnAxis(ap=index[0:n, :], axis=0),
                        bounds_check=N - 1, oob_is_err=False).then_inc(s, 16)

                def rows_to(s, table, index, of, n):
                    pool.indirect_dma_start(
                        table, bass.IndirectOffsetOnAxis(ap=index[0:n, :], axis=0), of[0:n, :], None,
                        bounds_check=N - 1, oob_is_err=False).then_inc(s, 16)

                def maxima_tile(t, n):
                    tile_stage(pool, s_maxima, MAXIMA, t, "gather")
                    rows_of(s_max_rows, gx[:, 0:D], x, src_i, n)
                    rows_of(s_max_rows, max_old, max_dram[:, :], dst_i, n)
                    tile_stage(pool, s_maxima, MAXIMA, t, "save")
                    rows_to(s_max_rows, max_dram[:, :], to_i, max_new, n)
                    wait_apart(pool, s_max_rows, t, MAXIMA_ROWS, MAXIMA_ROWS)

                def sums_tile(t, n):
                    tile_stage(pool, s_sums, SUMS, t, "gather")
                    rows_of(s_sum_rows, gx[:, 0:D], x, src_i, n)
                    rows_of(s_sum_rows, max_old, max_dram[:, :], dst_i, n)
                    rows_of(s_sum_rows, old, sum_dram[:, :], dst_i, n)
                    tile_stage(pool, s_sums, SUMS, t, "save")
                    rows_to(s_sum_rows, sum_dram[:, :], to_i, new, n)
                    wait_apart(pool, s_sum_rows, t, SUMS_ROWS, SUMS_ROWS)

                def nodes_tile(t, n):
                    tile_stage(pool, s_nodes, NODES, t, "root")
                    pool.tensor_tensor(rstd_c[0:n, :], var_c[0:n, :], power[0:n, 0:1], ALU.pow)\
                        .then_inc(s_nodes, 1)

                pool.wait_ge(s_clear, CLEARED)
                pool.memset(mv_c, 0.0).then_inc(s_maxima, 1)
                edge_tiles(pool, maxima_tile)
                pool.wait_ge(s_maxima, MAXIMA["all"] * (EDGE_TILES + 1) + 1)
                pool.memset(mv_c, 0.0).then_inc(s_sums, 1)
                edge_tiles(pool, sums_tile)
                pool.wait_ge(s_sums, SUMS["all"] * (EDGE_TILES + 1) + 1)
                pool.memset(mv_c, 0.0).then_inc(s_nodes, 1)
                node_tiles(pool, nodes_tile)

        @block.scalar
        def _(act):
            act.wait_ge(s_const, 11)
            for i, values in enumerate((dst, src)):
                for rows, part in windows_of(values):
                    act.dma_start(ds_table[rows, i * P:(i + 1) * P], part).then_inc(s_dst_tab, 16)
            blocks = G[:, :, :].rearrange("p a (b d) -> p (a b) d", d=P)
            for c in range(NECH):
                act.wait_ge(s_turn, c + 1)
                if c >= 2:
                    act.wait_ge(s_edot, c - 1)
                act.copy(turned_edges(c), turning[c % 2][:, 0:EPE * P]).then_inc(s_turned, 1)
                if c < ZERO_STEPS:
                    act.activation(blocks[:, c * ZERO_BLOCKS:(c + 1) * ZERO_BLOCKS, :],
                                   ones_sq[:, :].unsqueeze(1).broadcast_to([P, ZERO_BLOCKS, P]),
                                   ACT.Copy, scale=0.0).then_inc(s_gzero, 1)
                if c == WT_AT:
                    act.wait_ge(s_pe0, 6)
                    act.copy(WT[:, :, :], R[0][:, :].rearrange("p (c d) -> p c d", c=KC)).then_inc(s_WT, 1)
                if c == DWIN_AT:
                    act.wait_ge(s_dr, 1)
                    act.dma_start(dwin_dram[:, :].rearrange("(k p) e -> p k e", p=TR), dr[0:TR, :, :])\
                        .then_inc(s_dwin, 16)
                if c == DWIN_AT + 4:
                    act.wait_ge(s_dwin, 16)
                    act.dma_start(dwin[:, :, :], dwin_dram[:, :].rearrange("(b p) e -> p b e", p=BATCH))\
                        .then_inc(s_dwin2, 16)
            act.wait_ge(s_cready, 3)
            act.dma_start(c_lin[:, 0:EC * P].rearrange("a (p e) -> p (a e)", e=EC), c_out[:, :])\
                .then_inc(s_cstore, 16)
            act.dma_start(c_lin[:, EC * P:E].rearrange("a (p e) -> p (a e)", e=1), c_rest[:, 1:2],
                          allow_slow_non_contiguous=True).then_inc(s_cstore, 16)
            act.wait_ge(s_cstore, 32)
            for rows, part in windows_of(c_lin[:, :]):
                act.dma_start(c_table[rows, :], part).then_inc(s_ctab, 16)
            def exponentials(b):
                wait(act, s_shift, b, 1, 1)
                act.activation(w[:, :], shifted[:, :], ACT.Exp).then_inc(s_exp, 1)

            def evacuate(b, j):
                wait(act, s_agg, b, BATCH, j + 1)
                wait(act, s_proj, b, BATCH, j - 1)
                act.copy(AT[:, j % 2, :, :], A[j % 2][:, 0:D].rearrange("p (c n) -> p c n", c=KC))\
                    .then_inc(s_AT, 1)

            def weights(b, half, j):
                if j == 0 or j == BATCH:
                    wait(act, s_ready, b, 1, 1 + j // BATCH)
                wait(act, s_agg, b, BATCH, j - 3)
                k = j % BATCH
                act.activation(M[:, j % 4, :], F[:, half * BATCH + k, :], ACT.Copy,
                               scale=alpha_cur[:, half, k:k + 1]).then_inc(s_M, 1)

            def bias_rows(b, half, g):
                wait(act, s_edges, b, GROUPS, g + 1)
                wait(act, s_proj, b, BATCH, (g - 1) * GROUP)
                act.activation(bias_on[:, (half + g) % 2, :], edges6, ACT.Relu, bias=1.0, scale=-1.0)\
                    .then_inc(s_bias, 1)

            def iteration(b, half, use):
                first, last = isinstance(b, int) and b == 0, isinstance(b, int) and b == NBATCH - 1
                tiles = LAST_USED if last else BATCH
                for j in range(LAST_USED + LAG_APPLY if last else BATCH):
                    if j == EXP_SLOT and not last:
                        exponentials(b + 1)
                    if j + LEAD < tiles or not last:
                        weights(b, half if j + LEAD < BATCH else 1 - half, j + LEAD)
                    if j + 1 < tiles or not last:
                        evacuate(b, j + 1)
                    if j - LAG_APPLY >= 0 or not first:
                        t = (j - LAG_APPLY) % BATCH
                        if t % GROUP == 0:
                            wait(act, s_offset, b, GROUPS, (j - LAG_APPLY) // GROUP + 1)
                        tile = X[:, t // GROUP, t % GROUP, :]
                        act.activation(tile, tile, ACT.Identity, bias=nmr[:, t:t + 1],
                                       scale=rstd[:, t:t + 1]).then_inc(s_apply, 1)
                    if j % GROUP == 1 and (j < 24 or not last):
                        bias_rows(b, half, j // GROUP + 1)

            with act.If(windows_fit(act)):
                exponentials(0)
                weights(0, 0, 0)
                weights(0, 0, 1)
                bias_rows(0, 0, 0)
                evacuate(0, 0)
                batches(act, iteration)
            with act.Else():
                def sums_tile(t, n):
                    tile_stage(act, s_sums, SUMS, t, "spread")
                    act.activation(w_c[0:n, :], shift_c[0:n, :], ACT.Exp).then_inc(s_sums, 1)

                edge_tiles(act, sums_tile)

        @block.tensor
        def _(pe):
            def dot(o, lhs, rhs):
                for c in range(KC):
                    mm = pe.matmul(o, lhs[:, c, :], rhs[:, c, :], start=(c == 0), stop=(c == KC - 1))
                mm.then_inc(s_pe0, 1)

            pe.wait_ge(s_const, 11)
            pe.wait_ge(s_attn, 1)
            pe.matmul(R[1][:, 0:FIRST_ROWS], ones_row[:, :], firsts[:, :], start=True, stop=True)\
                .then_inc(s_pe0, 1)
            pe.wait_ge(s_attn, 3)
            dot(A[0][:, 0:KE], attn_rep, We_sb)
            for c in range(KC):
                mm = pe.matmul(A[0][:, KE:KE + 1], We_sb[:, c, :], attn_c[:, c:c + 1], start=(c == 0),
                               stop=(c == KC - 1))
            mm.then_inc(s_pe0, 1)

            def edge_terms(loads):
                for c in loads:
                    if c < NECH:
                        pe.wait_ge(s_ea[c % ERING], 16 * (c // ERING + 1))
                        if c >= 2:
                            pe.wait_ge(s_turned, c - 1)
                        for e in range(EPE):
                            mm = pe.transpose(turning[c % 2][:, e * P:(e + 1) * P],
                                              ea[:, c % ERING, e, :], ident[:, :])
                        mm.then_inc(s_turn, 1)
                    if c >= 1:
                        pe.wait_ge(s_turned, c)
                        for e in range(EPE):
                            at = (c - 1) * EPE + e
                            mm = pe.matmul(pe_terms[:, at:at + 1],
                                           turned_edges(c - 1)[:, e * P:(e + 1) * P], v_col[:, :],
                                           start=True, stop=True)
                        mm.then_inc(s_edot, 1)

            pe.wait_ge(s_v, 2)
            pe.wait_ge(s_rowidx, 1)
            edge_terms(range(0, WEIGHTS_AT + 1))
            pe.wait_ge(s_attn, 4)
            dot(A[1][:, 0:D], attn_rep, Wn_sb)
            for c in range(KC):
                mm = pe.matmul(R[3][:, 0:1], attn_rep[:, c, :], bne[:, c:c + 1], start=(c == 0),
                               stop=(c == KC - 1))
            mm.then_inc(s_pe0, 1)
            for k in range(KC):
                for c in range(KC):
                    mm = pe.transpose(R[0][:, k * D + c * P:k * D + (c + 1) * P],
                                      Wn_sb[:, c, k * P:(k + 1) * P], ident[:, :])
            mm.then_inc(s_pe0, 1)
            edge_terms(range(WEIGHTS_AT + 1, TURN_AT))
            pe.wait_ge(s_dr, 1)
            for k in range(TB):
                mm = pe.transpose(pS[:, k * TR:(k + 1) * TR], dr[0:TR, k, :], ident[0:TR, 0:TR])
            mm.then_inc(s_pe0, 1)
            edge_terms(range(TURN_AT, SRC_AT))
            pe.wait_ge(s_srcm, 1)
            for k in range(TB):
                mm = pe.transpose(R[2][:, k * TR:(k + 1) * TR], far[0:TR, k, :], ident[0:TR, 0:TR])
            mm.then_inc(s_pe0, 1)
            edge_terms(range(SRC_AT, FLAG_AT))
            pe.wait_ge(s_wrong, 1)
            pe.matmul(R[3][0:1, 4:7], ones_col[:, :], wrong[:, :], start=True, stop=True).then_inc(s_pe0, 1)
            edge_terms(range(FLAG_AT, NECH + 1))

            def count_edges(b, half, g):
                wait(pe, s_F, b, BATCH, (g + 1) * GROUP)
                wait(pe, s_bias, b, GROUPS, g)
                first_tile = half * BATCH + g % GROUPS * GROUP
                pe.matmul(edges6, pick6[:, :], F[:, first_tile:first_tile + GROUP, :],
                          start=True, stop=True).then_inc(s_edges, 1)

            def turn_scores(b):
                pe.transpose(scoreT, score[:, :], ident[:, :]).then_inc(s_scoreT, 1)

            def turn_alphas(b):
                pe.transpose(alphaT, alpha[:, :], ident[0:BATCH, 0:BATCH]).then_inc(s_alphaT, 1)

            def aggregate(b, half, j):
                wait(pe, s_M, b, BATCH, j + 1)
                wait(pe, s_AT, b, BATCH, j - 1)
                for c in range(KC):
                    mm = pe.matmul(A[j % 2][:, c * P:(c + 1) * P],
                                   G[:, half * BATCH + j % BATCH, c * P:(c + 1) * P], M[:, j % 4, :],
                                   start=True, stop=True)
                mm.then_inc(s_agg, 1)

            def project(b, half, j):
                wait(pe, s_AT, b, BATCH, j + 1)
                wait(pe, s_y, b, BATCH, j - 3)
                if j % GROUP == 0:
                    wait(pe, s_bias, b, GROUPS, j // GROUP + 1)
                o, at = projected(j), j % GROUP * P
                pe.matmul(o, bias_on[:, (half + j // GROUP) % 2, at:at + P], bn6[:, :],
                          start=True, stop=False)
                for c in range(KC):
                    mm = pe.matmul(o, AT[:, j % 2, c, :], WT[:, c, :], start=False, stop=(c == KC - 1))
                mm.then_inc(s_proj, 1)

            def iteration(b, half, use):
                last = isinstance(b, int) and b == NBATCH - 1
                for j in range(LAST_USED if last else BATCH):
                    if j == TURN_SLOT and not last:
                        wait(pe, s_score, b, BATCH, 2 * BATCH)
                    if j == ALPHA_SLOT and not last:
                        wait(pe, s_alpha, b, 1, 2)
                    if j % GROUP == 0 and (j < 24 or not last):
                        g = j // GROUP + 1
                        count_edges(b, half if g < GROUPS else 1 - half, g)
                    if j + 1 < LAST_USED or not last:
                        aggregate(b, half if j + 1 < BATCH else 1 - half, j + 1)
                    if j == TURN_SLOT and not last:
                        turn_scores(b + 1)
                    if j == ALPHA_SLOT and not last:
                        turn_alphas(b + 1)
                    project(b, half, j)

            with pe.If(windows_fit(pe)):
                count_edges(0, 0, 0)
                pe.wait_ge(s_score, BATCH)
                turn_scores(0)
                pe.wait_ge(s_alpha, 1)
                turn_alphas(0)
                pe.wait_ge(s_bn6, 16 * 2 * PARTS)
                pe.wait_ge(s_WT, 1)
                aggregate(0, 0, 0)
                batches(pe, iteration)
            with pe.Else():
                spread, total, turned, projection = A[0], A[1], R[0], R[1]
                pe.wait_ge(s_clear, 4)
                pe.matmul(spread[:, 0:D], ones_row[:, :], bn_row[:, :], start=True, stop=True)\
                    .then_inc(s_clear, 1)

                def maxima_tile(t, n):
                    tile_stage(pe, s_maxima, MAXIMA, t, "spread")
                    pe.matmul(spread[0:n, 0:2 * n], ones_sq[0:n, 0:n], diag[0:n, 0:2 * n], start=True,
                              stop=True).then_inc(s_maxima, 1)

                def sums_tile(t, n):
                    tile_stage(pe, s_sums, SUMS, t, "spread")
                    pe.matmul(spread[0:n, 0:n], ones_sq[0:n, 0:n], diag[0:n, 0:n], start=True,
                              stop=True).then_inc(s_sums, 1)
                    tile_stage(pe, s_sums, SUMS, t, "sum")
                    pe.matmul(total[0:n, 0:D + 1], masked[0:n, 0:n], gx[0:n, :], start=True, stop=True)\
                        .then_inc(s_sums, 1)

                def nodes_tile(t, n):
                    tile_stage(pe, s_nodes, NODES, t, "turn")
                    for c in range(KC):
                        mm = pe.transpose(turned[:, c * P:c * P + n], new[0:n, c * P:(c + 1) * P],
                                          ident[0:n, 0:n])
                    mm.then_inc(s_nodes, 1)
                    tile_stage(pe, s_nodes, NODES, t, "project")
                    for c in range(KC):
                        mm = pe.matmul(projection[0:n, 0:D], AT[:, 0, c, 0:n], WT[:, c, :],
                                       start=(c == 0), stop=(c == KC - 1))
                    mm.then_inc(s_nodes, 1)

                edge_tiles(pe, maxima_tile)
                edge_tiles(pe, sums_tile)
                node_tiles(pe, nodes_tile)

        @block.vector
        def _(dve):
            steps = [0]

            def link(instruction):
                steps[0] += 1
                instruction.then_inc(dve_step, 1)
                dve.wait_ge(dve_step, steps[0])

            def edge_terms(loads):
                for c in loads:
                    dve.wait_ge(s_ea[c % ERING], 16 * (c // ERING + 1))
                    for e in range(EPE, ECH):
                        part = ea[:, c % ERING, e, :]
                        ins = dve.tensor_tensor_reduce(
                            out=part, in0=part, in1=v_bc[:, :], scale=1.0, scalar=0.0, op0=ALU.mult,
                            op1=ALU.add, accum_out=c_main[:, c * ECH + e:c * ECH + e + 1])
                    ins.then_inc(s_ttr, 1)

            def ones_and_scores(b, half, use, tiles):
                for k in tiles:
                    dve.tensor_scalar(F[:, half * BATCH + k, :], iota_bf[:, :],
                                      drel_cur[:, half, k:k + 1], None, ALU.is_equal).then_inc(s_F, 1)
                    if k % GROUP == 0:
                        wait(dve, s_gather[half][k // GROUP], use, 16 * GROUP, 16 * GROUP)
                    dve.tensor_tensor_reduce(
                        out=junk[:, k % JUNK, :], in0=G[:, half * BATCH + k, :], in1=u_bc[:, :],
                        scale=1.0, scalar=0.0, op0=ALU.mult, op1=ALU.add,
                        accum_out=score[:, k:k + 1]).then_inc(s_score, 1)

            def first_scores(tiles):
                for k in tiles:
                    if k >= JUNK:
                        dve.wait_ge(s_score, k - JUNK + 1)
                    ones_and_scores(0, 0, 0, [k])

            dve.wait_ge(s_const, 11)
            dve.tensor_copy(iota_f[:, :], iota_i[:, :]).then_inc(dve_step, 1)
            dve.tensor_copy(iota_bf[:, :], iota_i[:, :]).then_inc(dve_step, 1)
            dve.memset(wrong[:, :], 0.0).then_inc(dve_step, 1)
            dve.memset(cont[:, 0:1], 0.0).then_inc(dve_step, 1)
            dve.memset(cont[:, P:P + 1], 0.0).then_inc(dve_step, 1)
            steps[0] += 5
            link(dve.tensor_copy(node0[:, :], node0_i[:, :]))
            dve.wait_ge(s_first, 16)
            dve.tensor_copy(firsts[:, :], firsts_i[:, :]).then_inc(s_attn, 1)
            dve.wait_ge(s_vload, 32)
            for c in range(KC):
                dve.tensor_scalar(attn_rep[:, c, :], ones_bf[:, :], attn_c[:, c:c + 1], None, ALU.mult)\
                    .then_inc(s_attn, 1)
            dve.wait_ge(s_pe0, 1)
            for k in range(TB):
                ins = dve.tensor_scalar(below[0:TR, k, 0:FIRST_ROWS], R[1][0:TR, 0:FIRST_ROWS],
                                        node0[0:TR, k:k + 1], None, ALU.is_lt, ALU.add,
                                        accum_out=nrows[0:TR, k:k + 1])
            link(ins)
            link(dve.tensor_scalar(row_f[0:TR, :], nrows[0:TR, :], -1.0, 0.0, ALU.add, ALU.max))
            dve.tensor_copy(row_i[0:TR, :], row_f[0:TR, :]).then_inc(s_rowidx, 1)
            dve.wait_ge(s_pe0, 3)
            dve.tensor_copy(v_bc[:, :], A[0][:, 0:KE]).then_inc(s_v, 1)
            dve.tensor_copy(v_col[:, :], A[0][:, KE:KE + 1]).then_inc(s_v, 1)
            dve.wait_ge(s_v, 1)
            edge_terms(range(0, WEIGHTS_AT))
            dve.wait_ge(s_wload, 64)
            dve.tensor_tensor(bne[:, :], bn_c[:, :], be_c[:, :], ALU.add).then_inc(s_attn, 1)
            edge_terms(range(WEIGHTS_AT, 6))
            dve.wait_ge(s_rows, 16 * TB)
            link(dve.tensor_copy(rows_f[0:TR, :, :], rows_i[0:TR, :, :]))
            for k in range(TB):
                ins = dve.tensor_scalar(below[0:TR, k, :], rows_f[0:TR, k, :], node0[0:TR, k:k + 1],
                                        None, ALU.is_lt, ALU.add, accum_out=nin[0:TR, k:k + 1])
            link(ins)
            link(dve.scalar_tensor_tensor(out=start_f[0:TR, :], in0=row_f[0:TR, :],
                                          scalar=float(FIRST_COLS), in1=nin[0:TR, :],
                                          op0=ALU.mult, op1=ALU.add))
            link(dve.tensor_copy(start_i[0:TR, :], start_f[0:TR, :]))
            link(dve.tensor_scalar(start_s[0:TR, :], start_i[0:TR, :], 4, None, ALU.arith_shift_right))
            link(dve.tensor_copy(start_sf[0:TR, :], start_s[0:TR, :]))
            link(dve.tensor_scalar(late[0:TR, :], start_f[0:TR, :], float(LATE), None, ALU.is_ge))
            link(dve.scalar_tensor_tensor(out=win_f[0:TR, :], in0=start_sf[0:TR, :],
                                          scalar=float(WROWS - 2), in1=late[0:TR, :],
                                          op0=ALU.min, op1=ALU.add))
            dve.tensor_copy(win_i[0:TR, :], win_f[0:TR, :]).then_inc(s_winidx, 1)
            edge_terms(range(6, 13))
            dve.wait_ge(s_win, 16 * TB)
            for k in range(TB):
                ins = dve.tensor_scalar(dr[0:TR, k, :], dsw[0:TR, k, 0:P], node0[0:TR, k:k + 1], None,
                                        ALU.subtract)
            steps[0] += 1
            ins.then_inc(dve_step, 1)
            dve.wait_ge(dve_step, steps[0])
            dve.tensor_scalar(away[0:TR, :, :], dr[0:TR, :, :], 0.0, float(FAR), ALU.is_lt, ALU.mult)\
                .then_inc(s_dr, 1)
            link(dve.tensor_scalar(far[0:TR, :, :], dr[0:TR, :, :], float(P), float(FAR), ALU.is_ge,
                                   ALU.mult))
            link(dve.tensor_tensor(away[0:TR, :, :], away[0:TR, :, :], far[0:TR, :, :], ALU.add))
            dve.tensor_tensor(far[0:TR, :, :], away[0:TR, :, :], dsw[0:TR, :, P:2 * P], ALU.add)\
                .then_inc(s_srcm, 1)
            edge_terms(range(13, 17))
            dve.wait_ge(s_pe0, 8)
            dve.tensor_copy(drel[:, :], pS[:, 0:TILES]).then_inc(dve_step, 1)
            steps[0] += 1
            dve.tensor_copy(srcidx[:, 0:TILES], R[2][:, 0:TILES]).then_inc(s_srcidx, 1)

            dve.wait_ge(s_pe0, 5)
            dve.tensor_copy(u_bc[:, :], A[1][:, 0:D]).then_inc(dve_step, 1)
            dve.tensor_copy(const_c[:, :], R[3][:, 0:1]).then_inc(dve_step, 1)
            steps[0] += 2
            link(dve.tensor_copy(bn_part[:, 0, :], bn_row[:, :]))
            link(dve.tensor_tensor(bn_rest[:, 0, :], bn_row[:, :], bn_part[:, 0, :], ALU.subtract))
            link(dve.tensor_copy(bn_part[:, 1, :], bn_rest[:, 0, :]))
            link(dve.tensor_tensor(bn_rest[:, 1, :], bn_rest[:, 0, :], bn_part[:, 1, :], ALU.subtract))
            link(dve.tensor_copy(bn_part[:, 2, :], bn_rest[:, 1, :]))
            dve.tensor_scalar(bn_part[:, PARTS:2 * PARTS, :], bn_part[:, 0:PARTS, :], -1.0, None, ALU.mult)\
                .then_inc(s_bnp, 1)
            edge_terms(range(17, CHECK_AT))
            link(dve.tensor_scalar(full[0:TR, 0, :], dr[0:TR, :, P - 1], float(P), None, ALU.is_lt))
            link(dve.scalar_tensor_tensor(out=full[0:TR, 1, :], in0=win_f[0:TR, :],
                                          scalar=float(WROWS - 1), in1=full[0:TR, 0, :],
                                          op0=ALU.is_lt, op1=ALU.mult))
            dve.tensor_reduce(wrong[0:TR, 0:1], full[0:TR, 1, :], AX.X, ALU.add).then_inc(dve_step, 1)
            steps[0] += 1
            dve.wait_ge(s_order, 32)
            dve.tensor_copy(orest_f[:, :], orest_i[:, :]).then_inc(dve_step, 1)
            steps[0] += 1
            link(dve.tensor_copy(order_f[:, :], order_i[:, :]))
            dve.tensor_tensor(vrest[:, 1:EREST], orest_f[:, 0:EREST - 1], orest_f[:, 1:EREST], ALU.is_gt)\
                .then_inc(dve_step, 1)
            steps[0] += 1
            link(dve.tensor_tensor(viol[:, :], order_f[:, 0:EC], order_f[:, 1:EC + 1], ALU.is_gt))
            dve.tensor_reduce(wrong[0:1, 2:3], vrest[:, 1:EREST], AX.X, ALU.add).then_inc(dve_step, 1)
            steps[0] += 1
            link(dve.tensor_reduce(wrong[:, 1:2], viol[:, :], AX.X, ALU.add))
            dve.tensor_copy(drel_cur[:, 0, :], drel[:, 0:BATCH]).then_inc(s_wrong, 1)
            dve.wait_ge(s_wrong, 1)

            for c in range(CHECK_AT, NECH - 2):
                edge_terms([c])
                if c >= SCORES_AT:
                    first_scores([c - SCORES_AT])
                if c == FLAG_AT:
                    dve.wait_ge(s_pe0, 9)
                    link(dve.tensor_reduce(wrong1[:, :], R[3][0:1, 4:7], AX.X, ALU.add))
                    dve.tensor_scalar(flag[:, :], wrong1[:, :], 1.0, None, ALU.min).then_inc(s_flag, 1)
                    dve.wait_ge(s_flag, 1)

            dve.wait_ge(s_ea_rest, 16)
            link(dve.tensor_tensor_reduce(out=ea_rest[:, :], in0=ea_rest[:, :], in1=v_bc[0:EREST, :],
                                          scale=1.0, scalar=0.0, op0=ALU.mult, op1=ALU.add,
                                          accum_out=c_rest[:, 0:1]))
            dve.tensor_scalar(c_rest[:, 1:2], c_rest[:, 0:1], const_c[0:EREST, 0:1], None, ALU.add)\
                .then_inc(s_cready, 1)
            edge_terms(range(NECH - 2, NECH))
            by_load = c_out[:, :].rearrange("p (c e) -> p c e", e=ECH)
            main = c_main[:, :].rearrange("p (c e) -> p c e", e=ECH)
            dve.wait_ge(s_ttr, NECH)
            dve.tensor_scalar(by_load[:, :, EPE:ECH], main[:, :, EPE:ECH], const_c[:, 0:1], None, ALU.add)\
                .then_inc(s_cready, 1)
            dve.wait_ge(s_edot, NECH)
            dve.tensor_scalar(by_load[:, :, 0:EPE], pe_terms.rearrange("p (c e) -> p c e", e=EPE),
                              const_c[:, 0:1], None, ALU.add).then_inc(s_cready, 1)
            first_scores(range(NECH - 2 - SCORES_AT, BATCH))
            dve.wait_ge(s_dwin2, 16)

            def window(t, b, at, n=P):
                if isinstance(b, int):
                    return t[:, b, at:at + n]
                return t[:, bass.ds(b, 1), at:at + n].rearrange("p a e -> p (a e)")

            def backward(part):
                return part[:, ::-1]

            def softmax(b, parts):
                def after(i):
                    wait(dve, s_soft, b, 10, i)

                if "masks" in parts:
                    dve.tensor_tensor(cont[:, 1:P], window(dwin, b, 1, P - 1), window(dwin, b, 0, P - 1),
                                      ALU.is_equal).then_inc(s_soft, 1)
                    after(1)
                    dve.tensor_scalar(neg[:, :], cont[:, :], -1.0, BIG, ALU.add, ALU.mult)\
                        .then_inc(s_soft, 1)
                if "scores" in parts:
                    wait(dve, s_scoreT, b, 1, 1)
                    dve.tensor_tensor(z[:, :], scoreT, window(cwin, b, 0), ALU.add).then_inc(s_soft, 1)
                    after(3)
                    dve.scalar_tensor_tensor(out=a[:, :], in0=z[:, :], scalar=SLOPE, in1=z[:, :],
                                             op0=ALU.mult, op1=ALU.max).then_inc(s_soft, 1)
                if "maximum" in parts:
                    after(4)
                    dve.tensor_tensor_scan(runmax[:, :], neg[:, 0:P], a[:, :], -BIG, ALU.add, ALU.max)\
                        .then_inc(s_soft, 1)
                    after(5)
                    dve.tensor_tensor_scan(backward(segmax), backward(neg[:, 1:P + 1]),
                                           backward(runmax), -BIG, ALU.add, ALU.max)\
                        .then_inc(s_soft, 1)
                    after(6)
                    dve.tensor_tensor(shifted[:, :], a[:, :], segmax[:, :], ALU.subtract)\
                        .then_inc(s_shift, 1)
                if "sum" in parts:
                    wait(dve, s_exp, b, 1, 1)
                    dve.tensor_tensor_scan(runsum[:, :], cont[:, 0:P], w[:, :], 0.0, ALU.mult, ALU.add)\
                        .then_inc(s_soft, 1)
                    after(7)
                    dve.tensor_tensor_scan(backward(segsum), backward(cont[:, 1:P + 1]),
                                           backward(runsum), 0.0, ALU.mult, ALU.max)\
                        .then_inc(s_soft, 1)
                    after(8)
                    dve.tensor_scalar(denom[:, :], segsum[:, :], 1e-16, None, ALU.add)\
                        .then_inc(s_soft, 1)
                    after(9)
                    dve.reciprocal(rdenom[:, :], denom[:, :]).then_inc(s_soft, 1)
                    after(10)
                    dve.tensor_tensor(alpha[:, :], w[:, :], rdenom[:, :], ALU.mult).then_inc(s_alpha, 1)

            def columns(b, half):
                wait(dve, s_alphaT, b, 1, 1)
                dve.tensor_copy(alpha_cur[:, half, :], alphaT).then_inc(s_ready, 1)

            def iteration(b, half, use):
                first, last = isinstance(b, int) and b == 0, isinstance(b, int) and b == NBATCH - 1
                tiles = LAST_USED if last else BATCH
                if not last:
                    if isinstance(b, int):
                        cols = drel[:, (b + 1) * BATCH:(b + 2) * BATCH]
                    else:
                        cols = drel[:, bass.ds((b + 1) * BATCH, BATCH)]
                    dve.tensor_copy(drel_cur[:, 1 - half, :], cols).then_inc(s_drel, 1)
                for j in range(BATCH + LAG_OFFSET if last else BATCH):
                    if not last:
                        if j == 0:
                            wait(dve, s_drel, b, 1, 1)
                        if j == COLUMNS:
                            columns(b + 1, 1 - half)
                        ones_and_scores(b + 1, 1 - half, use + half, scored(j))
                        if j == MASKS_SLOT:
                            softmax(b + 1, ("masks",))
                        if j == SOFT0:
                            if first:
                                dve.wait_ge(s_cwin2, 16)
                            softmax(b + 1, ("scores",))
                        if j == SOFT1:
                            softmax(b + 1, ("maximum",))
                        if j == SOFT2:
                            softmax(b + 1, ("sum",))
                    if (j >= 1 or not first) and (j - 1 < tiles or not last):
                        t = (j - 1) % BATCH
                        wait(dve, s_proj, b, BATCH, j)
                        if t % GROUP == 0 and j >= 1:
                            g = t // GROUP
                            wait(dve, s_xin[g], b, 16, 32 if last and g == GROUPS - 1 else 16)
                        tile = X[:, t // GROUP, t % GROUP, :]
                        dve.scalar_tensor_tensor(out=tile, in0=projected(t), scalar=0.0, in1=tile,
                                                 op0=ALU.max, op1=ALU.add).then_inc(s_y, 1)
                    g = (j - LAG_VAR) // GROUP
                    n, cols = group_columns(last, g)
                    if (j - LAG_VAR) % GROUP == 0 and (g >= 0 or not first) and g < GROUPS:
                        wait(dve, s_mv, b, BATCH, g * GROUP + n)
                        dve.tensor_scalar(var_e[:, cols], mv[:, cols, 1], EPS, None, ALU.add)\
                            .then_inc(s_var, 1)
                    g = (j - LAG_OFFSET) // GROUP
                    n, cols = group_columns(last, g)
                    if (j - LAG_OFFSET) % GROUP == 0 and (g >= 0 or not first) and g < GROUPS:
                        wait(dve, s_rstd, b, GROUPS, g + 1)
                        dve.scalar_tensor_tensor(out=nmr[:, cols], in0=mv[:, cols, 0], scalar=-1.0,
                                                 in1=rstd[:, cols], op0=ALU.mult, op1=ALU.mult)\
                            .then_inc(s_offset, 1)
                    if (j >= 2 or not first) and (j - 2 < tiles or not last):
                        t = (j - 2) % BATCH
                        wait(dve, s_y, b, BATCH, j - 1)
                        if not isinstance(b, int):
                            wait(dve, s_stats, b, BATCH, j - 2)
                        dve.bn_stats(stats[:, t % 4, :], X[:, t // GROUP, t % GROUP, :])\
                            .then_inc(s_stats, 1)
                    if (j >= 3 or not first) and (j - 3 < tiles or not last):
                        t = (j - 3) % BATCH
                        if isinstance(b, int):
                            wait(dve, s_stats, b, BATCH, j - 2)
                        dve.bn_aggr(mv[:, t, :], stats[:, t % 4, :]).then_inc(s_mv, 1)

            with dve.If(windows_fit(dve)):
                softmax(0, ("masks",))
                dve.wait_ge(s_cwin0, 16)
                softmax(0, ("scores", "maximum", "sum"))
                columns(0, 0)
                batches(dve, iteration)
            with dve.Else():
                dve.wait_ge(s_cwin0, 16)
                dve.wait_ge(s_cwin2, 16)
                dve.wait_ge(s_clear, 5)
                dve.tensor_copy(bn_bc, A[0][:, 0:D]).then_inc(s_clear, 1)
                dve.tensor_scalar(earlier, iota_f[:, :], float(P), node0[:, 0:1], ALU.mult, ALU.is_lt)\
                    .then_inc(s_clear, 1)

                def match(step, n):
                    step(lambda: dve.tensor_scalar(same[0:n, 0:n], A[0][0:n, 0:n], dst_f[0:n, :], None,
                                                   ALU.is_equal))
                    step(lambda: dve.tensor_tensor_reduce(
                        out=penalty[0:n, 0:n], in0=same[0:n, 0:n], in1=earlier[0:n, 0:n], scale=1.0,
                        scalar=0.0, op0=ALU.mult, op1=ALU.add, accum_out=count_c[0:n, :]))
                    step(lambda: dve.tensor_scalar(taken_c[0:n, :], count_c[0:n, :], 0.0, float(FAR),
                                                   ALU.is_gt, ALU.mult))
                    step(lambda: dve.tensor_tensor(to_c[0:n, :], taken_c[0:n, :], dst_f[0:n, :], ALU.add))
                    step(lambda: dve.tensor_copy(to_i[0:n, :], to_c[0:n, :]))

                def maxima_tile(t, n):
                    wait_apart(dve, s_max_rows, t, MAXIMA_ROWS, MAXIMA_GATHERED)
                    step = tile_steps(dve, s_maxima, MAXIMA, t, "score")
                    step(lambda: dve.tensor_copy(dst_f[0:n, :], dst_i[0:n, :]))
                    step(lambda: dve.tensor_tensor_reduce(
                        out=y[0:n, :], in0=gx[0:n, 0:D], in1=u_bc[0:n, :], scale=1.0, scalar=0.0,
                        op0=ALU.mult, op1=ALU.add, accum_out=score_c[0:n, :]))
                    step(lambda: dve.tensor_tensor(z_c[0:n, :], score_c[0:n, :], term_c[0:n, :], ALU.add))
                    step(lambda: dve.scalar_tensor_tensor(out=a_c[0:n, :], in0=z_c[0:n, :], scalar=SLOPE,
                                                          in1=z_c[0:n, :], op0=ALU.mult, op1=ALU.max))
                    step(lambda: dve.tensor_scalar(diag[0:n, 0:n], ident[0:n, 0:n], dst_f[0:n, :], None,
                                                   ALU.mult))
                    step(lambda: dve.tensor_scalar(diag[0:n, n:2 * n], ident[0:n, 0:n], a_c[0:n, :], None,
                                                   ALU.mult))
                    step = tile_steps(dve, s_maxima, MAXIMA, t, "maximum")
                    match(step, n)
                    step(lambda: dve.tensor_tensor(masked[0:n, 0:n], A[0][0:n, n:2 * n], same[0:n, 0:n],
                                                   ALU.mult))
                    step(lambda: dve.tensor_scalar(penalty[0:n, 0:n], same[0:n, 0:n], -1.0, BIG, ALU.add,
                                                   ALU.mult))
                    step(lambda: dve.tensor_tensor(masked[0:n, 0:n], masked[0:n, 0:n], penalty[0:n, 0:n],
                                                   ALU.add))
                    step(lambda: dve.tensor_reduce(max_loc[0:n, :], masked[0:n, 0:n], AX.X, ALU.max))
                    step(lambda: dve.tensor_tensor(max_new[0:n, :], max_loc[0:n, :], max_old[0:n, :],
                                                   ALU.max))

                def sums_tile(t, n):
                    wait_apart(dve, s_sum_rows, t, SUMS_ROWS, SUMS_GATHERED)
                    step = tile_steps(dve, s_sums, SUMS, t, "shift")
                    step(lambda: dve.tensor_copy(dst_f[0:n, :], dst_i[0:n, :]))
                    step(lambda: dve.tensor_scalar(diag[0:n, 0:n], ident[0:n, 0:n], dst_f[0:n, :], None,
                                                   ALU.mult))
                    step(lambda: dve.tensor_tensor(shift_c[0:n, :], a_c[0:n, :], max_old[0:n, :],
                                                   ALU.subtract))
                    step = tile_steps(dve, s_sums, SUMS, t, "match")
                    match(step, n)
                    step(lambda: dve.tensor_scalar(masked[0:n, 0:n], same[0:n, 0:n], w_c[0:n, :], None,
                                                   ALU.mult))
                    step = tile_steps(dve, s_sums, SUMS, t, "add")
                    step(lambda: dve.tensor_tensor(new[0:n, :], A[1][0:n, 0:D + 1], old[0:n, :], ALU.add))

                def nodes_tile(t, n):
                    step = tile_steps(dve, s_nodes, NODES, t, "divide")
                    weight = old[0:n, D:D + 1]
                    step(lambda: dve.tensor_scalar(den_c[0:n, :], weight, 1e-16, None, ALU.add))
                    step(lambda: dve.reciprocal(rden_c[0:n, :], den_c[0:n, :]))
                    step(lambda: dve.tensor_tensor(has_c[0:n, :], weight, rden_c[0:n, :], ALU.mult))
                    step(lambda: dve.tensor_scalar(new[0:n, 0:D], old[0:n, 0:D], rden_c[0:n, :], None,
                                                   ALU.mult))
                    step(lambda: dve.tensor_scalar(bias[0:n, :], bn_bc[0:n, :], has_c[0:n, :], None,
                                                   ALU.mult))
                    step = tile_steps(dve, s_nodes, NODES, t, "copy")
                    step(lambda: dve.tensor_copy(
                        AT[:, 0, :, 0:n],
                        R[0][:, 0:D].rearrange("p (c n) -> p c n", c=KC)[:, :, 0:n]))
                    step = tile_steps(dve, s_nodes, NODES, t, "norm")
                    step(lambda: dve.tensor_tensor(y[0:n, :], R[1][0:n, 0:D], bias[0:n, :], ALU.add))
                    step(lambda: dve.scalar_tensor_tensor(out=y[0:n, :], in0=y[0:n, :], scalar=0.0,
                                                          in1=xrow[0:n, :], op0=ALU.max, op1=ALU.add))
                    step(lambda: dve.bn_stats(stats_c[0:n, :], y[0:n, :]))
                    step(lambda: dve.bn_aggr(mv_c[0:n, :], stats_c[0:n, :]))
                    step(lambda: dve.tensor_scalar(var_c[0:n, :], mv_c[0:n, 1:2], EPS, None, ALU.add))
                    step = tile_steps(dve, s_nodes, NODES, t, "apply")
                    step(lambda: dve.tensor_scalar(y[0:n, :], y[0:n, :], mv_c[0:n, 0:1], rstd_c[0:n, :],
                                                   ALU.subtract, ALU.mult))

                edge_tiles(dve, maxima_tile)
                edge_tiles(dve, sums_tile)
                node_tiles(dve, nodes_tile)


_INS = ["x", "src", "dst", "edge_attr_128", "L0_gnn_Wn", "L0_gnn_bn", "L0_gnn_We", "L0_gnn_be", "L0_gnn_attn"]


def kernel(**inputs):
    import concourse.bacc as bacc
    from concourse.bass_utils import run_bass_kernel_spmd

    nc = bacc.Bacc("TRN2", target_bir_lowering=False, num_devices=1)
    arrays, args = {}, []
    for name in _INS:
        array = np.ascontiguousarray(inputs[name])
        arrays[f"in_{name}"] = array
        args.append(nc.dram_tensor(f"in_{name}", array.shape, mybir.dt.from_np(array.dtype),
                                   kind="ExternalInput").ap())
    out = nc.dram_tensor("out", (N, D), F32, kind="ExternalOutput").ap()
    gnn_kernel(nc, *args, out)
    result = run_bass_kernel_spmd(nc, [arrays], core_ids=[0])
    return result.results[0]["out"]
```
